# Optimizing a Trainium2 kernel written in Bass

```python
import numpy as np
import jax
import jax.numpy as jnp

def _softmax(x, axis=-1):
    return jax.nn.softmax(x, axis=axis)

def _gelu(x):
    return jax.nn.gelu(x, approximate=True)

def _silu(x):
    return jax.nn.silu(x)

def _sigmoid(x):
    return jax.nn.sigmoid(x)

def _layernorm(x, axis=-1, eps=1e-05):
    m = jnp.mean(x, axis=axis, keepdims=True)
    v = jnp.var(x, axis=axis, keepdims=True)
    return (x - m) / jnp.sqrt(v + eps)

def _scatter_add(tgt, idx, src, axis=0):
    return tgt.at[idx].add(src)

def _segment_sum(src, seg, n):
    return jax.ops.segment_sum(src, seg, n)
kernel_name = 'mk_metaformer_d1_conv_nchw256_r4_01f3b1'

def setup_inputs(seed: int=0):
    np.random.seed(seed)
    _w = jnp.asarray

    def _rec_inputs():
        import jax
        import jax.numpy as jnp
        _gk = jax.random.key(seed)
        x = -0.000125 + 0.9999 * jax.random.normal(jax.random.fold_in(_gk, 1), (8, 64, 32, 32), jnp.float32)
        return x
    x = _rec_inputs()

    def _L0_conv_setup():
        import jax, jax.numpy as jnp
        import numpy as np
        B, C, H, W = (8, 64, 32, 32)
        HEADS = 8
        key = jax.random.key(seed)
        k1, k2, k3, k4, k5 = jax.random.split(key, 5)
        x = jax.random.normal(k1, (B, C, H, W), dtype=jnp.float32)
        Wqkv = jax.random.normal(k2, (3 * C, C), dtype=jnp.float32) * C ** (-0.5)
        bqkv = jax.random.normal(k3, (3 * C,), dtype=jnp.float32) * 0.01
        Wout = jax.random.normal(k4, (C, C), dtype=jnp.float32) * C ** (-0.5)
        bout = jax.random.normal(k5, (C,), dtype=jnp.float32) * 0.01
        return {'x': x, 'Wqkv': Wqkv, 'bqkv': bqkv, 'Wout': Wout, 'bout': bout, 'num_heads': HEADS}
    _L0_conv_all = _L0_conv_setup()
    _L0_conv_in = {k: v for k, v in _L0_conv_all.items() if k in ('Wqkv', 'bqkv', 'Wout', 'bout')}
    del _L0_conv_all

    def _L0_ffn_setup():
        import math
        import jax, jax.numpy as jnp
        import numpy as np
        CAPACITY_FACTOR = 1.25
        TOP_K = 2
        LN_EPS = 1e-05

        def _layer_norm(x, gamma, beta):
            mu = jnp.mean(x, axis=-1, keepdims=True)
            var = jnp.var(x, axis=-1, keepdims=True)
            return (x - mu) * jax.lax.rsqrt(var + LN_EPS) * gamma + beta
        key = jax.random.key(seed)
        ks = jax.random.split(key, 4)
        B, S, D, F, E = (8, 1024, 64, 128, 8)
        x = jax.random.normal(ks[0], (B, S, D), dtype=jnp.float32)
        Wr = jax.random.normal(ks[1], (D, E), dtype=jnp.float32) / np.sqrt(D)
        br = jnp.zeros((E,), jnp.float32)
        W1 = jax.random.normal(ks[2], (E, D, F), dtype=jnp.float32) / np.sqrt(D)
        b1 = jnp.zeros((E, F), jnp.float32)
        W2 = jax.random.normal(ks[3], (E, F, D), dtype=jnp.float32) / np.sqrt(F)
        b2 = jnp.zeros((E, D), jnp.float32)
        gamma = jnp.ones((D,), jnp.float32)
        beta = jnp.zeros((D,), jnp.float32)
        return {'x': x, 'Wr': Wr, 'br': br, 'W1': W1, 'b1': b1, 'W2': W2, 'b2': b2, 'gamma': gamma, 'beta': beta}
    _L0_ffn_all = _L0_ffn_setup()
    _L0_ffn_in = {k: v for k, v in _L0_ffn_all.items() if k in ('Wr', 'br', 'W1', 'b1', 'W2', 'b2', 'gamma', 'beta')}
    del _L0_ffn_all
    return {'x': x, 'L0_conv_Wqkv': _L0_conv_in['Wqkv'], 'L0_conv_bqkv': _L0_conv_in['bqkv'], 'L0_conv_Wout': _L0_conv_in['Wout'], 'L0_conv_bout': _L0_conv_in['bout'], 'L0_ffn_Wr': _L0_ffn_in['Wr'], 'L0_ffn_br': _L0_ffn_in['br'], 'L0_ffn_W1': _L0_ffn_in['W1'], 'L0_ffn_b1': _L0_ffn_in['b1'], 'L0_ffn_W2': _L0_ffn_in['W2'], 'L0_ffn_b2': _L0_ffn_in['b2'], 'L0_ffn_gamma': _L0_ffn_in['gamma'], 'L0_ffn_beta': _L0_ffn_in['beta']}

def reference(x, L0_conv_Wqkv, L0_conv_bqkv, L0_conv_Wout, L0_conv_bout, L0_ffn_Wr, L0_ffn_br, L0_ffn_W1, L0_ffn_b1, L0_ffn_W2, L0_ffn_b2, L0_ffn_gamma, L0_ffn_beta):
    import jax
    import jax.numpy as jnp

    def _L0_conv_ref(x, Wqkv, bqkv, Wout, bout, num_heads):
        import jax, jax.numpy as jnp
        import numpy as np
        B, C, H, W = (8, 64, 32, 32)
        HEADS = 8
        b, c, h, w = x.shape
        n = h * w
        d = c // num_heads
        scale = d ** (-0.5)
        xf = x.reshape(b, c, n)
        qkv = jnp.einsum('oc,bcn->bon', Wqkv, xf) + bqkv[:, None]
        qkv = qkv.reshape(b, 3, num_heads, d, n)
        q, k, v = (qkv[:, 0] * scale, qkv[:, 1], qkv[:, 2])
        attn = jax.nn.softmax(jnp.einsum('bhdn,bhen->bhde', q, k), axis=-1)
        o = jnp.einsum('bhde,bhen->bhdn', attn, v)
        o = o.transpose(0, 2, 1, 3).reshape(b, c, n)
        out = jnp.einsum('oc,bcn->bon', Wout, o) + bout[:, None]
        return out.reshape(b, c, h, w)

    def _L0_ffn_ref(x, Wr, br, W1, b1, W2, b2, gamma, beta):
        import math
        import jax, jax.numpy as jnp
        import numpy as np
        CAPACITY_FACTOR = 1.25
        TOP_K = 2
        LN_EPS = 1e-05

        def _layer_norm(x, gamma, beta):
            mu = jnp.mean(x, axis=-1, keepdims=True)
            var = jnp.var(x, axis=-1, keepdims=True)
            return (x - mu) * jax.lax.rsqrt(var + LN_EPS) * gamma + beta
        B, S, D = x.shape
        E = Wr.shape[1]
        N = B * S
        K = TOP_K
        logits = jnp.mean(x, axis=1) @ Wr + br
        routing_weights = jax.nn.softmax(logits, axis=-1)
        capacity = float(math.ceil(N * CAPACITY_FACTOR / E))
        expected_loads = routing_weights.sum(axis=0) * (N / B)
        scale = jnp.where(expected_loads > capacity, capacity / expected_loads, 1.0)
        routing_weights = jax.nn.softmax(routing_weights * scale, axis=-1)
        rw_tok = jnp.broadcast_to(routing_weights[:, None, :], (B, S, E)).reshape(N, E)
        top_w, top_i = jax.lax.top_k(rw_tok, K)
        top_w = jax.nn.softmax(top_w, axis=-1)
        xf = x.reshape(N, D)
        h = jax.nn.gelu(jnp.einsum('nd,edf->enf', xf, W1) + b1[:, None, :], approximate=False)
        y = jnp.einsum('enf,efd->end', h, W2) + b2[:, None, :]
        w_dense = jnp.zeros((N, E), x.dtype).at[jnp.arange(N)[:, None], top_i].add(top_w)
        out = jnp.einsum('ne,end->nd', w_dense, y).reshape(B, S, D)
        out = _layer_norm(out + x, gamma, beta)
        return out

    def _gn(v, G=32, eps=1e-05):
        B_, C_, H_, W_ = v.shape
        g = v.reshape(B_, G, C_ // G, H_, W_)
        m = jnp.mean(g, axis=(2, 3, 4), keepdims=True)
        s = jnp.var(g, axis=(2, 3, 4), keepdims=True)
        return ((g - m) / jnp.sqrt(s + eps)).reshape(v.shape)

    def _ln_c(v, eps=1e-06):
        m = jnp.mean(v, axis=1, keepdims=True)
        s = jnp.var(v, axis=1, keepdims=True)
        return (v - m) / jnp.sqrt(s + eps)

    def _ln_t(v, eps=1e-05):
        m = jnp.mean(v, axis=-1, keepdims=True)
        s = jnp.var(v, axis=-1, keepdims=True)
        return (v - m) / jnp.sqrt(s + eps)

    def _to_tokens(v):
        B_, C_, H_, W_ = v.shape
        return v.reshape(B_, C_, H_ * W_).transpose(0, 2, 1)

    def _from_tokens(t, like):
        B_, C_, H_, W_ = like.shape
        return t.transpose(0, 2, 1).reshape(B_, C_, H_, W_)
    x = x + _L0_conv_ref(_ln_c(x), L0_conv_Wqkv, L0_conv_bqkv, L0_conv_Wout, L0_conv_bout, 8)
    t = _to_tokens(x)
    t = t + _L0_ffn_ref(_ln_t(t), L0_ffn_Wr, L0_ffn_br, L0_ffn_W1, L0_ffn_b1, L0_ffn_W2, L0_ffn_b2, L0_ffn_gamma, L0_ffn_beta)
    x = _from_tokens(t, x)
    return x

_drawn_inputs = setup_inputs


def setup_inputs(seed=0):
    import zlib

    import numpy as np

    out = dict(_drawn_inputs(seed))
    spreads = {'L0_ffn_br': (0.0, 0.1),
     'L0_ffn_b1': (0.0, 0.459),
     'L0_ffn_b2': (0.0, 0.293),
     'L0_ffn_gamma': (1.0, 0.2),
     'L0_ffn_beta': (0.0, 0.1)}
    factors = {'L0_conv_bqkv': 3.757, 'L0_conv_bout': 8.0, 'L0_ffn_Wr': 8.0}
    for name, (base, spread) in spreads.items():
        noise = np.random.default_rng([zlib.crc32(name.encode()), seed]).standard_normal(out[name].shape)
        drawn = base * np.exp(spread * noise) if base else spread * noise
        out[name] = jnp.asarray(drawn.astype(out[name].dtype))
    for name, factor in factors.items():
        out[name] = (out[name] * factor).astype(out[name].dtype)
    return out
```

```python
from contextlib import ExitStack

import concourse.bass as bass
from concourse import mybir
from concourse.alu_op_type import AluOpType as ALU

F32 = mybir.dt.float32
F16 = mybir.dt.float16
BF16 = mybir.dt.bfloat16
U32 = mybir.dt.uint32
ACT = mybir.ActivationFunctionType
AX_X = mybir.AxisListType.X

P = 128
B, C, N = 8, 64, 1024
NP = B // 2
CH = N // P
G2 = 2 * CH
HALF = N // 2
HEADS = 8
D = C // HEADS
E, F = 8, 128
TOP = 2
CAPACITY = float(-(-(B * N * 5 // 4) // E))
EPS_C, EPS_T = 1e-6, 1e-5
S_U, S_W = 16.0, 64.0

_COLS = [("wT", 3 * C + E), ("wvT", C), ("woT", C), ("bk", C), ("b2T", E), ("b1T", E), ("br", E),
         ("bq", 1), ("bv", 1), ("bout", 1), ("gamma", 1), ("beta", 1)]
_CONS = [("ident", P), ("cen2", P), ("cend", P), ("mean2", 2), ("mask", C)]
_CONB = [("sel", CH * P), ("identb", P), ("cenr", C)]


def offsets(cols):
    at, out = 0, {}
    for name, n in cols:
        out[name] = (at, at + n)
        at += n
    return out, at


OFF_W, W_COLS = offsets(_COLS)
OFF_C, C_COLS = offsets(_CONS)
OFF_B, B_COLS = offsets(_CONB)


def build_program(nc, x, small, w12, consts, constb, out):
    xv = x.rearrange("(p b) c n -> (b c) p n", b=2) if len(x.shape) == 4 else x
    with ExitStack() as ctx:
        def sb(name, shape, dt=F32):
            return ctx.enter_context(nc.sbuf_tensor(name, shape, dt))

        def sem(name):
            return ctx.enter_context(nc.semaphore(name))

        wsm = sb("wsm", [P, W_COLS])
        cst = sb("cst", [P, C_COLS])
        cstb = sb("cstb", [P, B_COLS], BF16)
        w12_sb = sb("w12_sb", [P, E * F])
        X = sb("X", [P, NP, N])
        T = sb("T", [P, NP, N])
        UT = sb("UT", [P, 2, CH, P + 2])
        U = sb("U", [P, 2, N])
        SQ = sb("SQ", [P, 2, N])
        UF = sb("UF", [P, 2, N])
        HI = sb("HI", [P, NP, N], F16)
        LO = sb("LO", [P, NP, N], F16)
        ST = sb("ST", [P, B, N], F16)
        H = sb("H", [P, 2, 2, N])
        ZS = sb("ZS", [P, 2, N])
        V = sb("V", [P, 2, N])
        OUT = sb("OUT", [P, 2, N])
        wTc = sb("wTc", [P, 3 * C + E])
        wvc = sb("wvc", [P, C])
        bqs = sb("bqs", [P, 1])
        w1hl = sb("w1hl", [P, E, 2, F], F16)
        w2c = sb("w2c", [P, E * C])
        b2c = sb("b2c", [P, E])
        bst = sb("bst", [P, 2, G2, 6])
        cmp1 = sb("cmp1", [P, 2, 4, G2])
        rt1 = sb("rt1", [P, 2, G2])
        Gs = sb("Gs", [P, 2, C + 3])
        p1s = sb("p1s", [P, 2, C])
        vbs = sb("vbs", [P, 2, 2, C])
        sm = sb("sm", [P, 2, C])
        nmx = sb("nmx", [P, 2, 2])
        Ex = sb("Ex", [P, 2, C])
        ssum = sb("ssum", [P, 2, 2])
        A = sb("A", [P, 2, C])
        B1s = sb("B1s", [P, 2, C])
        MTs = sb("MTs", [P, 2, P])
        cbs = sb("cbs", [P, NP])
        cmp2 = sb("cmp2", [P, 2, 3, G2])
        r2 = sb("r2", [P, 2, G2])
        rsp = sb("rsp", [P, 2, G2])
        rd = sb("rd", [P, 2, 2, G2])
        R3 = sb("R3", [P, 2, 3, G2], BF16)
        RR = sb("RR", [3 * G2, 2, P], BF16)
        mhalf = sb("mhalf", [P, G2])
        su = sb("su", [P, NP])
        rout = sb("rout", [P, 6, B * E])
        rsm = sb("rsm", [P, 8, B])
        m8 = sb("m8", [P, B, 8])
        i8 = sb("i8", [P, B, 8], U32)
        wk = sb("wk", [P, B, TOP])
        w1g = sb("w1g", [P, 2, 2, TOP, 2, F], F16)
        w2g = sb("w2g", [P, 2, 2, TOP, C])
        b1g = sb("b1g", [P, 2, 2, TOP])
        b2g = sb("b2g", [P, 2, 2, TOP])
        c2 = sb("c2", [P, NP])

        def w(name, p0=0, p1=P):
            a, b = OFF_W[name]
            return wsm[p0:p1, a:b]

        def cf(name, p0=0, p1=P):
            a, b = OFF_C[name]
            return cst[p0:p1, a:b]

        def cb(name, p0=0, p1=P):
            a, b = OFF_B[name]
            return cstb[p0:p1, a:b]

        WQ, WK, WR = slice(0, C), slice(C, 2 * C), slice(3 * C, 3 * C + E)

        pA = ctx.enter_context(nc.psum_tensor("pA", [P, N], F32))
        pB = ctx.enter_context(nc.psum_tensor("pB", [P, N], F32))
        pC = ctx.enter_context(nc.psum_tensor("pC", [P, N], F32))
        pS = ctx.enter_context(nc.psum_tensor("pS", [P, HALF], F32))
        pM = ctx.enter_context(nc.psum_tensor("pM", [P, HALF], F32))
        xt, ut, rb, cv = pA, pB, pB, pC
        pR = pS
        h_ps, y_ps = [pA, pB], pC
        ps_g, ps_p1, ps_vb = pS[:, 0:C + 2], pS[:, 66:66 + C], pS[:, 130:130 + C]
        ps_s, ps_b1, ps_mt, ps_cb = pS[:, 194:194 + C], pS[:, 258:258 + C], pS[:, 322:322 + C], pS[:, 386:387]
        ps_m = pM[:, 0:2 * G2]
        ps_rt = pM[0:3 * G2, P:P + P // 2].bitcast(BF16)
        ps_lg = [pS[:, 0:NP * E], pC[:, 0:NP * E]]

        s_cst, s_cstb, s_wsm, s_w12 = sem("s_cst"), sem("s_cstb"), sem("s_wsm"), sem("s_w12")
        s_x = [sem(f"s_x{p}") for p in range(NP)]
        s_st = [sem(f"s_st{p}") for p in range(NP)]
        s_out = [sem(f"s_out{p}") for p in range(NP)]
        names = ("ones mh wcp wcv wvp wvv xt ut gram gs tb u p1 p1s s_ps sms exs a_sb b1 b1s mt mts conv t sq stat cmp2 pow1 "
                 "pow2 r3 rt rr rb uf hi lo b2p w1p w1h w1l w2p w2v lg rexp1 rexp2 rexp3 rx1 rx2 rx3 wkd top gat c2d "
                 "mm1 gelu mm2 zs sq3 stat3 cmp3 pow3 r33 rt3 rr3 rb3 v3 fin tbeta v1 "
                 "dve pool bns bnw").split()
        s = {n: sem("s_" + n) for n in names}

        block = ctx.enter_context(nc.Block())

        @block.sync
        def _(sp):
            sp.dma_start(X[:, 0, :], xv[:, 0, :]).then_inc(s_x[0], 16)
            sp.dma_start(cst[:, :], consts).then_inc(s_cst, 16)
            sp.dma_start(X[:, 1, :], xv[:, 1, :]).then_inc(s_x[1], 16)
            sp.dma_start(X[:, 2, :], xv[:, 2, :]).then_inc(s_x[2], 16)
            sp.dma_start(X[:, 3, :], xv[:, 3, :]).then_inc(s_x[3], 16)
            sp.dma_start(w12_sb[:, :], w12).then_inc(s_w12, 16)
            for p in range(NP):
                for half, src, done in ((0, HI, s["hi"]), (1, LO, s["lo"])):
                    sp.wait_ge(done, p + 1)
                    for b in range(2):
                        sp.dma_start(ST[half * C:(half + 1) * C, 2 * p + b, :],
                                     src[b * C:(b + 1) * C, p, :]).then_inc(s_st[p], 16)
            for p in range(NP):
                sp.wait_ge(s["fin"], p + 1)
                sp.dma_start(out[:, p, :], OUT[:, p % 2, :]).then_inc(s_out[p], 16)
            for p in range(NP):
                sp.wait_ge(s_out[p], 16)

        @block.scalar
        def _(act):
            act.dma_start(wsm[:, :], small).then_inc(s_wsm, 16)
            act.dma_start(cstb[:, :], constb).then_inc(s_cstb, 16)

            def evac_u(p):
                act.wait_ge(s["tb"], p + 1)
                if p >= 2:
                    act.wait_ge(s["conv"], p - 1)
                nc.scalar.copy(U[:, p % 2, :], ut[:, :]).then_inc(s["u"], 1)

            def softmax_exp(p):
                act.wait_ge(s["sms"], p + 1)
                if p >= 2:
                    act.wait_ge(s["a_sb"], p - 1)
                nc.scalar.activation(Ex[:, p % 2, :], sm[:, p % 2, :], ACT.Exp, bias=nmx[:, p % 2, 0:1],
                                     accum_out=ssum[:, p % 2, 0:1]).then_inc(s["exs"], 1)

            def square_t(p):
                act.wait_ge(s["t"], p + 1)
                if p >= 2:
                    act.wait_ge(s["stat"], p - 1)
                nc.scalar.activation(SQ[:, p % 2, :], T[:, p, :], ACT.Square).then_inc(s["sq"], 1)

            def round_hi(p):
                act.wait_ge(s["uf"], p + 1)
                nc.scalar.copy(HI[:, p, :], UF[:, p % 2, :]).then_inc(s["hi"], 1)

            for p in range(NP):
                evac_u(p)
                if p >= 1:
                    square_t(p - 1)
                softmax_exp(p)
                if p >= 1:
                    round_hi(p - 1)
            square_t(NP - 1)
            act.wait_ge(s["w1p"], 1)
            nc.scalar.mul(w1hl[:, :, 0, :], pA[:, :].rearrange("p (e f) -> p e f", e=E), S_W).then_inc(s["w1h"], 1)
            round_hi(NP - 1)
            for n in (1, 2, 3):
                act.wait_ge(s[f"rx{n}"], 1)
                src = {1: rout[:, 1, :], 2: rout[:, 4, :], 3: rsm[:, 6, :]}[n]
                dst = {1: rout[:, 2, :], 2: rout[:, 5, :], 3: rsm[:, 7, :]}[n]
                nc.scalar.activation(dst, src, ACT.Exp).then_inc(s[f"rexp{n}"], 1)

            def gelu(p, k, b):
                step = TOP * p + k
                act.wait_ge(s["mm1"], 2 * step + b + 1)
                if step >= 2:
                    act.wait_ge(s["mm2"], step - 1)
                nc.scalar.activation(H[:, step % 2, b, :], h_ps[b][:, :], ACT.Gelu,
                                     bias=b1g[:, p % 2, b, k:k + 1],
                                     scale=1.0 / (S_U * S_W)).then_inc(s["gelu"], 1)

            def square_z(p):
                act.wait_ge(s["zs"], p + 1)
                if p >= 2:
                    act.wait_ge(s["stat3"], p - 1)
                nc.scalar.activation(SQ[:, p % 2, :], ZS[:, p % 2, :], ACT.Square).then_inc(s["sq3"], 1)

            act.wait_ge(s["gat"], TOP * 2)
            for p in range(NP):
                if p >= 1:
                    act.wait_ge(s["gat"], TOP * 2 * (p + 1))
                for k in range(TOP):
                    for b in range(2):
                        gelu(p, k, b)
                    if k == 0 and p >= 1:
                        square_z(p - 1)
            square_z(NP - 1)

        @block.gpsimd
        def _(pool):
            count = [0]

            def link(ins):
                count[0] += 1
                ins.then_inc(s["pool"], 1)
                pool.wait_ge(s["pool"], count[0])

            nc.gpsimd.memset(mhalf[:, :], -0.5).then_inc(s["mh"], 1)
            nc.gpsimd.memset(UT[:, :, :, 0:P + 2:P + 1], 1.0).then_inc(s["ones"], 1)
            nc.gpsimd.memset(MTs[:, :, :], 0.0).then_inc(s["ones"], 1)
            pool.wait_ge(s["mh"], 1)

            def split3(p, src, ready, used, done):
                if p >= 2:
                    pool.wait_ge(used, p - 1)
                b = p % 2
                link(nc.gpsimd.tensor_copy(R3[:, b, 0, :], src))
                link(nc.gpsimd.tensor_tensor(rd[:, b, 0, :], src, R3[:, b, 0, :], ALU.subtract))
                link(nc.gpsimd.tensor_copy(R3[:, b, 1, :], rd[:, b, 0, :]))
                link(nc.gpsimd.tensor_tensor(rd[:, b, 1, :], rd[:, b, 0, :], R3[:, b, 1, :], ALU.subtract))
                nc.gpsimd.tensor_copy(R3[:, b, 2, :], rd[:, b, 1, :]).then_inc(done, 1)

            def rstd1(p):
                pool.wait_ge(s["v1"], p + 1)
                nc.gpsimd.tensor_tensor(rt1[:, p % 2, :], cmp1[:, p % 2, 3, :], mhalf[:, :],
                                        ALU.pow).then_inc(s["pow1"], 1)

            def rstd2(p):
                pool.wait_ge(s["cmp2"], p + 1)
                link(nc.gpsimd.tensor_tensor(r2[:, p % 2, :], cmp2[:, p % 2, 2, :], mhalf[:, :], ALU.pow))
                split3(p, r2[:, p % 2, :], None, s["rt"], s["r3"])

            def low(p):
                pool.wait_ge(s["uf"], p + 1)
                pool.wait_ge(s["hi"], p + 1)
                nc.gpsimd.tensor_tensor(LO[:, p, :], UF[:, p % 2, :], HI[:, p, :],
                                        ALU.subtract).then_inc(s["lo"], 1)

            rstd1(0)
            for p in range(NP):
                if p + 1 < NP:
                    rstd1(p + 1)
                if p >= 1:
                    rstd2(p - 1)
                    low(p - 1)
            rstd2(NP - 1)
            low(NP - 1)
            for p in range(NP):
                last = nc.gpsimd.tensor_scalar(T[:, p, :], T[:, p, :], w("beta"), None, ALU.add)
                last.then_inc(s["tbeta"], 1)

            pool.wait_ge(s["w1l"], 1)
            pool.wait_ge(s["w2v"], 2)
            pool.wait_ge(s["top"], 1)
            pool.wait_ge(s["wkd"], 1)

            def gather(p):
                if p >= 2:
                    pool.wait_ge(s["mm2"], TOP * (p - 1))
                    pool.wait_ge(s["gelu"], 2 * TOP * (p - 1))
                    pool.wait_ge(s["c2d"], p - 1)
                for k in range(TOP):
                    for b in range(2):
                        i = 2 * p + b
                        e = nc.gpsimd.value_load(i8[0:1, i, k:k + 1], min_val=0, max_val=E - 1)
                        wrep = wk[:, i, k:k + 1]
                        nc.gpsimd.tensor_copy(
                            w1g[:, p % 2, b, k, :, :].rearrange("p a f -> p (a f)").bitcast(F32),
                            w1hl[:, :, :, :].rearrange("p e a f -> p (e a f)").bitcast(F32)[:, bass.ds(e * F, F)])
                        nc.gpsimd.tensor_copy(b1g[:, p % 2, b, k:k + 1], w("b1T")[:, bass.ds(e, 1)])
                        nc.gpsimd.tensor_tensor(b2g[:, p % 2, b, k:k + 1], b2c[:, bass.ds(e, 1)], wrep, ALU.mult)
                        nc.gpsimd.tensor_tensor(w2g[:, p % 2, b, k, :], w2c[:, bass.ds(e * C, C)],
                                                wrep.broadcast_to([P, C]), ALU.mult).then_inc(s["gat"], 1)

            def rstd3(p):
                pool.wait_ge(s["cmp3"], p + 1)
                link(nc.gpsimd.tensor_tensor(r2[:, p % 2, :], rsp[:, p % 2, :], mhalf[:, :], ALU.pow))
                split3(p, r2[:, p % 2, :], None, s["rt3"], s["r33"])

            gather(0)
            gather(1)
            for p in range(NP):
                rstd3(p)
                if p + 2 < NP:
                    gather(p + 2)

        @block.vector
        def _(dve):
            count = [0]

            def link(ins):
                count[0] += 1
                ins.then_inc(s["dve"], 1)
                dve.wait_ge(s["dve"], count[0])

            def stats1(p):
                dve.wait_ge(s["xt"], p + 1)
                if p >= 2:
                    dve.wait_ge(s["pow1"], p - 1)
                q = p % 2
                for g in range(G2):
                    last = nc.vector.bn_stats(bst[:, q, g, :], xt[:, g * C:(g + 1) * C])
                link(last)
                me, ve, mo, vo = (bst[:, q, :, i] for i in (1, 2, 4, 5))
                nc.vector.tensor_tensor(cmp1[:, q, 1, :], ve, vo, ALU.add)
                link(nc.vector.tensor_tensor(cmp1[:, q, 0, :], me, mo, ALU.subtract))
                link(nc.vector.tensor_tensor(cmp1[:, q, 2, :], cmp1[:, q, 0, :], cmp1[:, q, 0, :], ALU.mult))
                link(nc.vector.scalar_tensor_tensor(out=cmp1[:, q, 0, :], in0=cmp1[:, q, 2, :], scalar=C / 4.0,
                                                    in1=cmp1[:, q, 1, :], op0=ALU.mult, op1=ALU.add))
                nc.vector.tensor_scalar(cmp1[:, q, 3, :], cmp1[:, q, 0, :], 1.0 / C, EPS_C, ALU.mult,
                                        ALU.add).then_inc(s["v1"], 1)

            def scale1(p):
                dve.wait_ge(s["pow1"], p + 1)
                if p >= 2:
                    dve.wait_ge(s["tb"], p - 1)
                q = p % 2
                nc.vector.tensor_tensor(
                    UT[:, q, :, 1:P + 1].rearrange("p j (b c) -> p j b c", b=2),
                    xt[:, :].rearrange("p (j b c) -> p j b c", b=2, c=C),
                    rt1[:, q, :].rearrange("p (j b) -> p j b", b=2).unsqueeze(3).broadcast_to([P, CH, 2, C]),
                    ALU.mult).then_inc(s["ut"], 1)

            def att_gram(p):
                q = p % 2
                dve.wait_ge(s["gram"], p + 1)
                if p >= 2:
                    dve.wait_ge(s["p1"], p - 1)
                link(nc.vector.tensor_copy(Gs[:, q, 0:C + 2], ps_g))
                nc.vector.tensor_tensor(Gs[:, q, C + 2:C + 3], Gs[:, q, 0:1], Gs[:, q, C + 1:C + 2],
                                        ALU.add).then_inc(s["gs"], 1)

            def att_p1(p):
                q = p % 2
                dve.wait_ge(s["gs"], p + 1)
                dve.wait_ge(s["p1"], p + 1)
                if p >= 2:
                    dve.wait_ge(s["s_ps"], p - 1)
                nc.vector.scalar_tensor_tensor(out=vbs[:, q, 0, :], in0=w("bk"), scalar=float(N), in1=ps_vb,
                                               op0=ALU.mult, op1=ALU.add)
                nc.vector.scalar_tensor_tensor(out=p1s[:, q, :], in0=w("bk"), scalar=Gs[:, q, C + 2:C + 3], in1=ps_p1,
                                               op0=ALU.mult, op1=ALU.add).then_inc(s["p1s"], 1)
                dve.wait_ge(s["p1s"], p + 1)
                link(nc.vector.scalar_tensor_tensor(out=vbs[:, q, 1, :], in0=vbs[:, q, 0, :], scalar=bqs[:, 0:1],
                                                    in1=cf("mask"), op0=ALU.mult, op1=ALU.add))

            def att_scores(p):
                q = p % 2
                dve.wait_ge(s["s_ps"], p + 1)
                if p >= 2:
                    dve.wait_ge(s["exs"], p - 1)
                link(nc.vector.tensor_tensor(sm[:, q, :], vbs[:, q, 1, :], ps_s, ALU.add))
                nc.vector.tensor_reduce(nmx[:, q, 0:1], sm[:, q, :], AX_X, ALU.max, negate=True).then_inc(s["sms"], 1)

            def att_probs(p):
                q = p % 2
                dve.wait_ge(s["exs"], p + 1)
                if p >= 2:
                    dve.wait_ge(s["b1"], p - 1)
                link(nc.vector.reciprocal(ssum[:, q, 1:2], ssum[:, q, 0:1]))
                nc.vector.tensor_scalar(A[:, q, :], Ex[:, q, :], ssum[:, q, 1:2], None,
                                        ALU.mult).then_inc(s["a_sb"], 1)

            def att_b1(p):
                q = p % 2
                dve.wait_ge(s["b1"], p + 1)
                if p >= 2:
                    dve.wait_ge(s["mt"], p - 1)
                nc.vector.tensor_copy(B1s[:, q, :], ps_b1).then_inc(s["b1s"], 1)

            def att_mt(p):
                q = p % 2
                dve.wait_ge(s["mt"], p + 1)
                dve.wait_ge(s["ones"], 2)
                if p >= 2:
                    dve.wait_ge(s["conv"], p - 1)
                nc.vector.tensor_copy(MTs[0:C, q, 0:C], ps_mt[0:C, :])
                nc.vector.tensor_copy(MTs[C:P, q, C:P], ps_mt[C:P, :])
                nc.vector.tensor_tensor(cbs[:, p:p + 1], w("bout"), ps_cb, ALU.add).then_inc(s["mts"], 1)

            def residual1(p):
                dve.wait_ge(s["conv"], p + 1)
                dve.wait_ge(s["mts"], p + 1)
                nc.vector.scalar_tensor_tensor(out=T[:, p, :], in0=cv[:, :], scalar=cbs[:, p:p + 1], in1=X[:, p, :],
                                               op0=ALU.add, op1=ALU.add).then_inc(s["t"], 1)

            def stats2(p):
                q = p % 2
                dve.wait_ge(s["stat"], p + 1)
                if p >= 2:
                    dve.wait_ge(s["r3"], p - 1)
                pm = ps_m.rearrange("p (a g) -> p a g", a=2)
                link(nc.vector.tensor_scalar(cmp2[:, q, 0, :], pm[:, 0, :], 1.0 / S_U, None, ALU.mult))
                link(nc.vector.tensor_tensor(cmp2[:, q, 1, :], cmp2[:, q, 0, :], cmp2[:, q, 0, :], ALU.mult))
                link(nc.vector.scalar_tensor_tensor(out=cmp2[:, q, 0, :], in0=pm[:, 1, :], scalar=1.0 / S_U ** 2,
                                                    in1=cmp2[:, q, 1, :], op0=ALU.mult, op1=ALU.subtract))
                nc.vector.tensor_scalar(cmp2[:, q, 2, :], cmp2[:, q, 0, :], EPS_T / S_U ** 2, None,
                                        ALU.add).then_inc(s["cmp2"], 1)

            def rows2(p):
                dve.wait_ge(s["rt"], p + 1)
                if p >= 2:
                    dve.wait_ge(s["rb"], p - 1)
                nc.vector.tensor_copy(RR[:, p % 2, :], ps_rt).then_inc(s["rr"], 1)

            def normal2(p):
                dve.wait_ge(s["rb"], p + 1)
                if p >= 2:
                    dve.wait_ge(s["hi"], p - 1)
                    dve.wait_ge(s["lo"], p - 1)
                nc.vector.scalar_tensor_tensor(out=UF[:, p % 2, :], in0=T[:, p, :], scalar=1.0, in1=rb[:, :],
                                               op0=ALU.mult, op1=ALU.mult,
                                               accum_out=su[:, p:p + 1]).then_inc(s["uf"], 1)

            dve.wait_ge(s["wcp"], 1)
            dve.wait_ge(s_wsm, 16)
            nc.vector.tensor_scalar(wTc[:, WQ], pS[:, 0:C], D ** -0.5, None, ALU.mult)
            nc.vector.tensor_copy(wTc[:, C:3 * C + E], pS[:, C:3 * C + E])
            nc.vector.tensor_scalar(bqs[:, :], w("bq"), D ** -0.5, None, ALU.mult)
            nc.vector.tensor_copy(b2c[:, :], pS[:, 260:260 + E])
            link(nc.vector.tensor_copy(wvc[:, :], pS[:, 300:300 + C]))
            nc.vector.memset(ps_g, 0.0).then_inc(s["wcv"], 1)
            stats1(0)
            scale1(0)
            for p in range(NP):
                att_gram(p)
                if p + 1 < NP:
                    stats1(p + 1)
                att_p1(p)
                att_scores(p)
                if p >= 1:
                    stats2(p - 1)
                att_probs(p)
                if p + 1 < NP:
                    scale1(p + 1)
                att_b1(p)
                if p >= 1:
                    rows2(p - 1)
                att_mt(p)
                if p >= 1:
                    normal2(p - 1)
                residual1(p)
            stats2(NP - 1)
            dve.wait_ge(s["w1p"], 1)
            dve.wait_ge(s["w1h"], 1)
            nc.vector.scalar_tensor_tensor(out=w1hl[:, :, 1, :], in0=pA[:, :].rearrange("p (e f) -> p e f", e=E),
                                           scalar=S_W, in1=w1hl[:, :, 0, :], op0=ALU.mult,
                                           op1=ALU.subtract).then_inc(s["w1l"], 1)
            dve.wait_ge(s["w2p"], 1)
            nc.vector.tensor_copy(w2c[:, :], pB[:, 0:E * C]).then_inc(s["w2v"], 2)
            rows2(NP - 1)
            normal2(NP - 1)

            def be(ap):
                return ap.rearrange("p (b e) -> p b e", e=E)

            def over_e(ap):
                return ap.unsqueeze(2).broadcast_to([P, B, E])

            dve.wait_ge(s["lg"], 1)
            for b in range(2):
                last = nc.vector.scalar_tensor_tensor(out=be(rout[:, 0, :])[:, b:B:2, :], in0=be(ps_lg[b]),
                                                      scalar=1.0 / (S_U * N),
                                                      in1=w("br").unsqueeze(1).broadcast_to([P, NP, E]),
                                                      op0=ALU.mult, op1=ALU.add)
            link(last)
            link(nc.vector.tensor_reduce(rsm[:, 0, :], be(rout[:, 0, :]), AX_X, ALU.max))
            nc.vector.tensor_tensor(be(rout[:, 1, :]), be(rout[:, 0, :]), over_e(rsm[:, 0, :]),
                                    ALU.subtract).then_inc(s["rx1"], 1)
            dve.wait_ge(s["rexp1"], 1)
            link(nc.vector.reduce_sum(rsm[:, 1, :], be(rout[:, 2, :]), AX_X))
            link(nc.vector.reciprocal(rsm[:, 2, :], rsm[:, 1, :]))
            link(nc.vector.tensor_tensor(be(rout[:, 0, :]), be(rout[:, 2, :]), over_e(rsm[:, 2, :]), ALU.mult))
            link(nc.vector.reduce_sum(rsm[:, 3, :], rout[:, 0, :].rearrange("p (b e) -> p e b", e=E), AX_X))
            link(nc.vector.reciprocal(rsm[:, 4, :], rsm[:, 3, :]))
            link(nc.vector.tensor_scalar(rsm[:, 5, :], rsm[:, 4, :], CAPACITY / N, 1.0, ALU.mult, ALU.min))
            link(nc.vector.tensor_tensor(be(rout[:, 3, :]), be(rout[:, 0, :]),
                                         rsm[:, 5, :].unsqueeze(1).broadcast_to([P, B, E]), ALU.mult))
            for i in range(B):
                last = nc.vector.max(m8[:, i, :], rout[:, 3, i * E:(i + 1) * E])
            link(last)
            nc.vector.tensor_tensor(be(rout[:, 4, :]), be(rout[:, 3, :]),
                                    m8[:, :, 0:1].broadcast_to([P, B, E]), ALU.subtract).then_inc(s["rx2"], 1)
            for i in range(B):
                last = nc.vector.max_index(i8[:, i, :], m8[:, i, :], rout[:, 3, i * E:(i + 1) * E])
            last.then_inc(s["top"], 1)
            dve.wait_ge(s["rexp2"], 1)
            link(nc.vector.reduce_sum(rsm[:, 0, :], be(rout[:, 5, :]), AX_X))
            link(nc.vector.reciprocal(rsm[:, 1, :], rsm[:, 0, :]))
            for i in range(B):
                last = nc.vector.max(m8[:, i, :], rout[:, 5, i * E:(i + 1) * E])
            link(last)
            link(nc.vector.tensor_scalar(rsm[:, 2, :], m8[:, :, 1], 1.0, None, ALU.subtract))
            nc.vector.tensor_tensor(rsm[:, 6, :], rsm[:, 2, :], rsm[:, 1, :], ALU.mult).then_inc(s["rx3"], 1)
            dve.wait_ge(s["rexp3"], 1)
            link(nc.vector.tensor_scalar(rsm[:, 3, :], rsm[:, 7, :], 1.0, None, ALU.add))
            link(nc.vector.reciprocal(wk[:, :, 0], rsm[:, 3, :]))
            nc.vector.tensor_tensor(wk[:, :, 1], wk[:, :, 0], rsm[:, 7, :], ALU.mult).then_inc(s["wkd"], 1)

            def bias2(p):
                dve.wait_ge(s["gat"], 2 * TOP * (p + 1))
                for b in range(2):
                    rows = slice(b * C, (b + 1) * C)
                    last = nc.vector.tensor_tensor(c2[rows, p:p + 1], b2g[rows, p % 2, b, 0:1],
                                                   b2g[rows, p % 2, b, 1:2], ALU.add)
                last.then_inc(s["c2d"], 1)

            def evac_z(p):
                dve.wait_ge(s["mm2"], TOP * (p + 1))
                dve.wait_ge(s["c2d"], p + 1)
                nc.vector.tensor_scalar(ZS[:, p % 2, :], y_ps[:, :], c2[:, p:p + 1], None,
                                        ALU.add).then_inc(s["zs"], 1)

            def stats3(p):
                dve.wait_ge(s["stat3"], p + 1)
                if p >= 2:
                    dve.wait_ge(s["r33"], p - 1)
                nc.vector.tensor_scalar(rsp[:, p % 2, :], ps_m[:, 0:G2], EPS_T, None, ALU.add).then_inc(s["cmp3"], 1)

            def rows3(p):
                dve.wait_ge(s["rt3"], p + 1)
                if p >= 2:
                    dve.wait_ge(s["rb3"], 2 * (p - 1))
                nc.vector.tensor_copy(RR[:, p % 2, :], ps_rt).then_inc(s["rr3"], 1)

            def finish(p):
                q = p % 2
                for h in range(2):
                    dve.wait_ge(s["rb3"], 2 * p + h + 1)
                    if h == 0:
                        dve.wait_ge(s["zs"], p + 1)
                    cols = slice(h * HALF, (h + 1) * HALF)
                    last = nc.vector.tensor_tensor(V[:, q, cols], ZS[:, q, cols], pR[:, :], ALU.mult)
                    last.then_inc(s["v3"], 1)
                dve.wait_ge(s["v3"], 2 * (p + 1))
                dve.wait_ge(s["tbeta"], p + 1)
                if p >= 2:
                    dve.wait_ge(s_out[p - 2], 16)
                nc.vector.scalar_tensor_tensor(out=OUT[:, q, :], in0=V[:, q, :], scalar=w("gamma"), in1=T[:, p, :],
                                               op0=ALU.mult, op1=ALU.add).then_inc(s["fin"], 1)

            bias2(0)
            bias2(1)
            for p in range(NP):
                evac_z(p)
                stats3(p)
                rows3(p)
                finish(p)
                if p + 2 < NP:
                    bias2(p + 2)

        @block.tensor
        def _(pe):
            mm = nc.tensor.matmul

            def half(ap, b):
                return ap[b * C:(b + 1) * C]

            def transpose_x(p):
                pe.wait_ge(s_x[p], 16)
                if p == 0:
                    pe.wait_ge(s_cst, 16)
                if p >= 1:
                    pe.wait_ge(s["ut"], p)
                for j in range(CH):
                    last = nc.tensor.transpose(xt[:, j * P:(j + 1) * P], X[:, p, j * P:(j + 1) * P], cf("ident"))
                last.then_inc(s["xt"], 1)

            def gram(p):
                q = p % 2
                pe.wait_ge(s["ut"], p + 1)
                pe.wait_ge(s["ones"], 2)
                if p >= 1:
                    pe.wait_ge(s["mts"], p)
                for j in range(CH):
                    for b in range(2):
                        last = mm(half(ps_g[:, b:b + C + 1], b), UT[:, q, j, 1 + b * C:1 + (b + 1) * C],
                                  UT[:, q, j, b * (C + 1):(b + 1) * (C + 1)],
                                  start=(j == 0), stop=(j == CH - 1))
                last.then_inc(s["gram"], 1)

            def transpose_u(p):
                q = p % 2
                if p >= 1:
                    pe.wait_ge(s["u"], p)
                if p >= 2:
                    pe.wait_ge(s["uf"], p - 1)
                for j in range(CH):
                    last = nc.tensor.transpose(ut[:, j * P:(j + 1) * P], UT[:, q, j, 1:P + 1], cf("ident"))
                last.then_inc(s["tb"], 1)

            def att_p1(p):
                q = p % 2
                pe.wait_ge(s["gs"], p + 1)
                pe.wait_ge(s["wcv"], 1)
                if p >= 1:
                    pe.wait_ge(s["sms"], p)
                for b in range(2):
                    mm(half(ps_p1, b), half(Gs[:, q, 1:C + 1], b), half(wTc[:, WK], b), start=True, stop=True)
                    last = mm(half(ps_vb, b), half(Gs[:, q, C + 2:C + 3], b).broadcast_to([C, C]),
                              half(wTc[:, WK], b), start=True, stop=True)
                last.then_inc(s["p1"], 1)

            def att_s(p):
                pe.wait_ge(s["p1s"], p + 1)
                for b in range(2):
                    last = mm(half(ps_s, b), half(wTc[:, WQ], b), half(p1s[:, p % 2, :], b), start=True, stop=True)
                last.then_inc(s["s_ps"], 1)

            def att_b1(p):
                pe.wait_ge(s["a_sb"], p + 1)
                if p >= 1:
                    pe.wait_ge(s["b1s"], p)
                for b in range(2):
                    last = mm(half(ps_b1, b), half(A[:, p % 2, :], b), half(w("woT"), b), start=True, stop=True)
                last.then_inc(s["b1"], 1)

            def att_mt(p):
                pe.wait_ge(s["b1s"], p + 1)
                if p >= 1:
                    pe.wait_ge(s["mts"], p)
                for b in range(2):
                    mm(half(ps_mt, b), half(wvc[:, :], b), half(B1s[:, p % 2, :], b), start=True, stop=True)
                    last = mm(half(ps_cb, b), half(B1s[:, p % 2, :], b), half(w("bv"), b), start=True, stop=True)
                last.then_inc(s["mt"], 1)

            def conv(p):
                pe.wait_ge(s["mts"], p + 1)
                pe.wait_ge(s["u"], p + 1)
                if p >= 1:
                    pe.wait_ge(s["t"], p)
                for h in range(2):
                    cols = slice(h * HALF, (h + 1) * HALF)
                    last = mm(cv[:, cols], MTs[:, p % 2, :], U[:, p % 2, cols], start=True, stop=True)
                last.then_inc(s["conv"], 1)

            def moments(p):
                pe.wait_ge(s["t"], p + 1)
                pe.wait_ge(s["sq"], p + 1)
                if p >= 1:
                    pe.wait_ge(s["rr"], p)
                for a, src in ((0, T[:, p, :]), (1, SQ[:, p % 2, :])):
                    for j in range(CH):
                        c0 = a * G2 + 2 * j
                        last = mm(ps_m[:, c0:c0 + 2], src[:, j * P:(j + 1) * P], cf("mean2"), start=True, stop=True)
                last.then_inc(s["stat"], 1)

            def rows(p, ready, read, done):
                pe.wait_ge(ready, p + 1)
                if p >= 1:
                    pe.wait_ge(read, p)
                nc.tensor.transpose(ps_rt, R3[:, p % 2, :, :].rearrange("p k g -> p (k g)"),
                                    cb("identb")).then_inc(done, 1)

            def spread2(p):
                pe.wait_ge(s["rr"], p + 1)
                pe.wait_ge(s["u"], min(p + 2, NP))
                for j in range(CH):
                    last = mm(rb[:, j * P:(j + 1) * P], cb("sel")[0:3 * G2, j * P:(j + 1) * P], RR[:, p % 2, :],
                              start=True, stop=True)
                last.then_inc(s["rb"], 1)

            def spread3(p):
                pe.wait_ge(s["rr3"], p + 1)
                for h in range(2):
                    if 2 * p + h >= 1:
                        pe.wait_ge(s["v3"], 2 * p + h)
                    for k in range(CH // 2):
                        j = h * CH // 2 + k
                        last = mm(pR[:, k * P:(k + 1) * P], cb("sel")[0:3 * G2, j * P:(j + 1) * P],
                                  RR[:, p % 2, :], start=True, stop=True)
                    last.then_inc(s["rb3"], 1)

            pe.wait_ge(s_cst, 16)
            pe.wait_ge(s_wsm, 16)
            mm(pS[:, 0:3 * C + E], cf("cen2"), w("wT"), start=True, stop=True)
            mm(pS[:, 260:260 + E], cf("cen2"), w("b2T"), start=True, stop=True)
            for b in range(2):
                last = mm(half(pS[:, 300:300 + C], b), half(w("wvT"), b), half(cf("cend"), b)[:, 0:C],
                          start=True, stop=True)
            last.then_inc(s["wcp"], 1)
            transpose_x(0)
            pe.wait_ge(s["wcv"], 1)
            pe.wait_ge(s_cstb, 16)
            gram(0)
            transpose_u(0)
            for p in range(NP):
                if p + 1 < NP:
                    transpose_x(p + 1)
                att_p1(p)
                att_s(p)
                if p >= 1:
                    moments(p - 1)
                att_b1(p)
                if p >= 1:
                    rows(p - 1, s["r3"], s["rr"], s["rt"])
                att_mt(p)
                if p >= 1:
                    spread2(p - 1)
                if p + 1 < NP:
                    gram(p + 1)
                conv(p)
                if p + 1 < NP:
                    transpose_u(p + 1)
            pe.wait_ge(s_w12, 16)
            for h in range(2):
                last = mm(pA[:, h * HALF:(h + 1) * HALF], cf("cend", 0, C), w12_sb[0:C, h * HALF:(h + 1) * HALF],
                          start=True, stop=True)
            last.then_inc(s["w1p"], 1)
            pe.wait_ge(s["uf"], NP - 1)
            pe.wait_ge(s["u"], NP)
            for e in range(E):
                last = mm(pB[:, e * C:(e + 1) * C], w12_sb[C:P, e * F:(e + 1) * F], cf("cend", C, P)[:, 0:C],
                          start=True, stop=True)
            last.then_inc(s["w2p"], 1)
            moments(NP - 1)
            rows(NP - 1, s["r3"], s["rr"], s["rt"])
            pe.wait_ge(s["w2v"], 2)
            spread2(NP - 1)
            pe.wait_ge(s["uf"], NP)
            for i in range(B):
                b = i % 2
                last = mm(ps_lg[b][:, i // 2 * E:(i // 2 + 1) * E], half(su[:, i // 2:i // 2 + 1], b).broadcast_to([C, P]),
                          half(wTc[:, WR], b), start=True, stop=True)
            last.then_inc(s["lg"], 1)

            def up(p, k):
                step = TOP * p + k
                if k == 0:
                    pe.wait_ge(s_st[p], 64)
                for b in range(2):
                    pe.wait_ge(s["gat"], 2 * TOP * p + 2 * k + b + 1)
                    if step >= 1:
                        pe.wait_ge(s["gelu"], 2 * (step - 1) + b + 1)
                    if step == 0:
                        pe.wait_ge(s["w1l"], 1)
                        pe.wait_ge(s["w2v"], 2)
                    for a in range(2):
                        for h in range(2):
                            cols = slice(h * HALF, (h + 1) * HALF)
                            last = mm(h_ps[b][:, cols], w1g[:, p % 2, b, k, a, :], ST[:, 2 * p + b, cols],
                                      start=(a == 0), stop=(a == 1))
                    last.then_inc(s["mm1"], 1)

            def down(p, k):
                step = TOP * p + k
                if k == 0:
                    if p >= 1:
                        pe.wait_ge(s["zs"], p)
                    for h in range(2):
                        cols = slice(h * HALF, (h + 1) * HALF)
                        for b in range(2):
                            mm(half(y_ps[:, cols], b), cb("cenr"), ST[:, 2 * p + b, cols], start=True, stop=False)
                pe.wait_ge(s["gelu"], 2 * (step + 1))
                for h in range(2):
                    cols = slice(h * HALF, (h + 1) * HALF)
                    for b in range(2):
                        last = mm(half(y_ps[:, cols], b), w2g[:, p % 2, b, k, :], H[:, step % 2, b, cols],
                                  start=False, stop=(k == TOP - 1))
                last.then_inc(s["mm2"], 1)

            def moments3(p):
                pe.wait_ge(s["sq3"], p + 1)
                pe.wait_ge(s["rr"], NP)
                if p >= 1:
                    pe.wait_ge(s["rr3"], p)
                for j in range(CH):
                    last = mm(ps_m[:, 2 * j:2 * j + 2], SQ[:, p % 2, j * P:(j + 1) * P], cf("mean2"),
                              start=True, stop=True)
                last.then_inc(s["stat3"], 1)

            for p in range(NP):
                up(p, 0)
                if p >= 1:
                    down(p - 1, 1)
                up(p, 1)
                if p >= 1:
                    moments3(p - 1)
                down(p, 0)
                if p >= 1:
                    rows(p - 1, s["r33"], s["rr3"], s["rt3"])
                    spread3(p - 1)
            down(NP - 1, 1)
            moments3(NP - 1)
            rows(NP - 1, s["r33"], s["rr3"], s["rt3"])
            spread3(NP - 1)


def kernel(x, L0_conv_Wqkv, L0_conv_bqkv, L0_conv_Wout, L0_conv_bout, L0_ffn_Wr, L0_ffn_br, L0_ffn_W1, L0_ffn_b1,
           L0_ffn_W2, L0_ffn_b2, L0_ffn_gamma, L0_ffn_beta):
    import ml_dtypes
    import numpy as np
    import concourse.bacc as bacc
    from concourse.bass_utils import run_bass_kernel_spmd

    def twice(a):
        a = np.asarray(a)
        return np.concatenate([a, a], axis=0)

    def rows(a):
        return np.broadcast_to(np.asarray(a)[None, :], (P, a.shape[0]))

    wqkv, bqkv, wout = np.asarray(L0_conv_Wqkv), np.asarray(L0_conv_bqkv), np.asarray(L0_conv_Wout)
    parts = {
        "wT": twice(np.concatenate([wqkv.T, np.asarray(L0_ffn_Wr)], axis=1)),
        "wvT": twice(wqkv[2 * C:].T), "woT": twice(wout.T.reshape(D, HEADS, C).transpose(1, 0, 2).reshape(C, C)), "bk": rows(bqkv[C:2 * C]),
        "b2T": twice(np.asarray(L0_ffn_b2).T), "b1T": np.asarray(L0_ffn_b1).T, "br": rows(L0_ffn_br),
        "bq": twice(bqkv[:C, None]), "bv": twice(bqkv[2 * C:, None]),
        "bout": twice(np.asarray(L0_conv_bout)[:, None]), "gamma": twice(np.asarray(L0_ffn_gamma)[:, None]),
        "beta": twice(np.asarray(L0_ffn_beta)[:, None]),
    }
    small = np.ascontiguousarray(np.concatenate([parts[n] for n, _ in _COLS], axis=1))
    w12 = np.ascontiguousarray(np.concatenate(
        [np.asarray(L0_ffn_W1).transpose(1, 0, 2).reshape(C, E * F),
         np.asarray(L0_ffn_W2).transpose(2, 0, 1).reshape(C, E * F)], axis=0))
    xin = np.ascontiguousarray(np.asarray(x).reshape(NP, P, N).transpose(1, 0, 2))

    eye = np.eye(C, dtype=np.float32)
    cen = eye - np.float32(1.0 / C)
    zero = np.zeros((C, C), np.float32)
    head = np.arange(P)[:, None] % C // D
    cons = {
        "ident": np.eye(P, dtype=np.float32), "cen2": np.block([[cen, zero], [zero, cen]]),
        "cend": np.block([[cen, cen], [cen, cen]]),
        "mean2": (np.arange(P)[:, None] // C == np.arange(2)[None, :]).astype(np.float32) / np.float32(C),
        "mask": np.where(head == np.arange(C)[None, :] // D, 0.0, -1e30).astype(np.float32),
    }
    consts = np.ascontiguousarray(np.concatenate([cons[n] for n, _ in _CONS], axis=1))
    sel = np.zeros((P, CH, P), np.float32)
    for k in range(3):
        for j in range(CH):
            for b in range(2):
                sel[k * G2 + 2 * j + b, j, b * C:(b + 1) * C] = 1.0
    conb = {"sel": sel.reshape(P, CH * P), "identb": np.eye(P, dtype=np.float32),
            "cenr": np.concatenate([cen, cen], axis=0) / np.float32(S_U)}
    constb = np.ascontiguousarray(np.concatenate([conb[n] for n, _ in _CONB], axis=1).astype(ml_dtypes.bfloat16))

    nc = bacc.Bacc("TRN2", target_bir_lowering=False, num_devices=1)
    arrays = {"x_dram": xin, "small_dram": small, "w12_dram": w12, "consts_dram": consts, "constb_dram": constb}
    args = [nc.dram_tensor(n, a.shape, mybir.dt.from_np(a.dtype), kind="ExternalInput").ap()
            for n, a in arrays.items()]
    args.append(nc.dram_tensor("out_dram", (P, NP, N), F32, kind="ExternalOutput").ap())
    build_program(nc, *args)
    r = run_bass_kernel_spmd(nc, [arrays], core_ids=[0])
    got = np.asarray(r.results[0]["out_dram"])
    return np.ascontiguousarray(got.transpose(1, 0, 2)).reshape(B, C, 32, 32)
```

```python
from contextlib import ExitStack

import concourse.bass as bass
from concourse import mybir
from concourse.alu_op_type import AluOpType as ALU

F32 = mybir.dt.float32
F16 = mybir.dt.float16
BF16 = mybir.dt.bfloat16
U32 = mybir.dt.uint32
ACT = mybir.ActivationFunctionType
AX_X = mybir.AxisListType.X

P = 128
B, C, N = 8, 64, 1024
NP = B // 2
CH = N // P
G2 = 2 * CH
HALF = N // 2
HEADS = 8
D = C // HEADS
E, F = 8, 128
TOP = 2
CAPACITY = float(-(-(B * N * 5 // 4) // E))
EPS_C, EPS_T = 1e-6, 1e-5
S_U, S_W = 16.0, 64.0

_COLS = [("wT", 3 * C + E), ("wvT", C), ("woT", C), ("bk", C), ("b2T", E), ("b1T", E), ("br", E),
         ("bq", 1), ("bv", 1), ("bout", 1), ("gamma", 1), ("beta", 1)]
_CONS = [("ident", P), ("cen2", P), ("cend", P), ("mean2", 32), ("mask", C)]
_CONB = [("sel", CH * P), ("identb", P), ("cenr", C)]


def offsets(cols):
    at, out = 0, {}
    for name, n in cols:
        out[name] = (at, at + n)
        at += n
    return out, at


OFF_W, W_COLS = offsets(_COLS)
OFF_C, C_COLS = offsets(_CONS)
OFF_B, B_COLS = offsets(_CONB)


def build_program(nc, x_tok, x_cha, small, w12, consts, constb, out):
    with ExitStack() as ctx:
        def sb(name, shape, dt=F32):
            return ctx.enter_context(nc.sbuf_tensor(name, shape, dt))

        def sem(name):
            return ctx.enter_context(nc.semaphore(name))

        wsm = sb("wsm", [P, W_COLS])
        cst = sb("cst", [P, C_COLS])
        cstb = sb("cstb", [P, B_COLS], BF16)
        w12_sb = sb("w12_sb", [P, E * F])
        XT = sb("XT", [P, NP, N])
        X = sb("X", [P, NP, N])
        T = sb("T", [P, NP, N])
        UT = sb("UT", [P, NP, CH, P + 2])
        U = sb("U", [P, NP, N])
        SQ = sb("SQ", [P, 2, N])
        UF = sb("UF", [P, NP, N])
        HI = sb("HI", [P, NP, N], F16)
        LO = sb("LO", [P, NP, N], F16)
        ST = sb("ST", [P, B, N], F16)
        H = sb("H", [P, 2, 2, N])
        ZS, V, OUT = U, XT, XT
        wTc = sb("wTc", [P, 3 * C + E])
        wvc = sb("wvc", [P, C])
        bqs = sb("bqs", [P, 1])
        w1hl = sb("w1hl", [P, E, 2, F], F16)
        w2c = sb("w2c", [P, E * C])
        b2c = sb("b2c", [P, E])
        bst = sb("bst", [P, 2, 2 * G2, 6])
        cmp1 = sb("cmp1", [P, 2, 4, 2 * G2])
        rt1 = sb("rt1", [P, 2, 2 * G2])
        Gs = sb("Gs", [P, 2, 2 * (P + 2)])
        p1s = sb("p1s", [P, 2, 2, C])
        vbs = sb("vbs", [P, 2, 2, 2, C])
        sm = sb("sm", [P, 2, 2, C])
        nmx = sb("nmx", [P, 2, 2])
        Ex = sb("Ex", [P, 2, 2, C])
        ssum = sb("ssum", [P, 2, 2, 2])
        A = sb("A", [P, 2, 2, C])
        B1s = sb("B1s", [P, 2, 2, C])
        MTs = sb("MTs", [P, NP, P])
        cbs = sb("cbs", [P, NP])
        RW = sb("RW", [P, 2, HALF])
        cmp2 = sb("cmp2", [P, 2, 4, 2 * G2])
        seed = sb("seed", [P, 2 * G2], U32)
        nwt = sb("nwt", [P, 3, 2 * G2])
        r2 = sb("r2", [P, NP, G2])
        r3 = sb("r3", [P, NP, G2])
        v3 = sb("v3", [P, NP, G2])
        rd = sb("rd", [P, 2, 2, G2])
        R3 = sb("R3", [P, 2, 3, G2], BF16)
        RR = sb("RR", [3 * G2, 2, P], BF16)
        su = sb("su", [P, NP])
        wrbd = sb("wrbd", [P, 2 * E])
        sw = sb("sw", [P, B * E])
        ones_m = sb("ones_m", [P, P])
        rout = sb("rout", [P, 4, B * E])
        rx = sb("rx", [P, 2, (E + 1) * B])
        rsm = sb("rsm", [P, 8, B])
        m8 = sb("m8", [P, B, 8])
        i8 = sb("i8", [P, B, 8], U32)
        wk = sb("wk", [P, B, TOP])
        w1g = sb("w1g", [P, 2, 2, TOP, 2, F], F16)
        w2g = sb("w2g", [P, 2, 2, TOP, C])
        b1g = sb("b1g", [P, 2, 2, TOP])
        b2g = sb("b2g", [P, 2, 2, TOP])
        c2 = sb("c2", [P, NP])
        gtab = sb("gtab", [P, 1])

        def w(name, p0=0, p1=P):
            a, b = OFF_W[name]
            return wsm[p0:p1, a:b]

        def cf(name, p0=0, p1=P):
            a, b = OFF_C[name]
            return cst[p0:p1, a:b]

        def cb(name, p0=0, p1=P):
            a, b = OFF_B[name]
            return cstb[p0:p1, a:b]

        def moments_of(bank):
            return bank.rearrange("p (s h q r) -> p s h q r", s=2, h=2, r=32)[:, :, :, :, 0:2]

        def by_half(ap):
            return ap.rearrange("p (q h b) -> p h q b", h=2, b=2)

        WQ, WK, WR = slice(0, C), slice(C, 2 * C), slice(3 * C, 3 * C + E)

        pA = ctx.enter_context(nc.psum_tensor("pA", [P, N], F32))
        pB = ctx.enter_context(nc.psum_tensor("pB", [P, N], F32))
        pC = ctx.enter_context(nc.psum_tensor("pC", [P, N], F32))
        pS = ctx.enter_context(nc.psum_tensor("pS", [P, HALF], F32))
        pM = ctx.enter_context(nc.psum_tensor("pM", [P, HALF], F32))
        ut, rb, cv = pA, [pC, pA], pC
        h_ps, y_ps, rb3 = [pA, pB], pC, pS
        G1 = P + 2
        small_bank = [pS, pB]

        def pair_view(ap):
            return ap.rearrange("p (l c) -> p l c", l=2)

        ps_g = [q[:, 0:2 * G1] for q in small_bank]
        ps_p1 = [pair_view(q[:, 260:388]) for q in small_bank]
        ps_vb = [pair_view(q[:, 0:128]) for q in small_bank]
        ps_s = [pair_view(q[:, 128:256]) for q in small_bank]
        ps_b1, ps_mt, ps_cb = ps_p1, ps_vb, [q[:, 388:390] for q in small_bank]
        moment_bank = [pM, pS]
        ps_w2 = pB[:, HALF:N]
        ps_rt2 = pB[0:3 * G2, 0:P].bitcast(BF16)
        ps_rt3 = pS[0:3 * G2, 0:P // 2].bitcast(BF16)
        ps_lg = pS[:, 0:B * E]

        s_cst, s_cstb, s_wsm, s_w12 = sem("s_cst"), sem("s_cstb"), sem("s_wsm"), sem("s_w12")
        s_xt = [sem(f"s_xt{p}") for p in range(NP)]
        s_x = [sem(f"s_x{p}") for p in range(NP)]
        s_ut = [sem(f"s_ut{p}") for p in range(NP)]
        s_fin = [sem(f"s_fin{i}") for i in range(B)]
        s_st = [sem(f"s_st{p}") for p in range(NP)]
        s_out = [sem(f"s_out{p}") for p in range(NP)]
        names = ("ones clear onesm wrb sw wcp wcv gram gs tb u p1 p1s s_ps sms exs a_sb b1 b1s mt mts cbs conv t sq row rw mom "
                 "v1 v2 pow1 pow2 red2 r3 rt rr rb uf hi lo w1p w1h w1l w2p w2v lg rexp1 rexp2 rexp3 rx1 rx2 rx3 wkd top "
                 "g1 g2 c2d mm1 gelu mm2 zs sq3 row3 rw3 mom3 red3 pow3 s3 rt3 rr3 rb3 vv tbeta dve pool").split()
        s = {n: sem("s_" + n) for n in names}

        KA = [2, 3, 2, 3, 3, 3, 2, 5, 4, 18, 0, 4, 22, 2, 14]
        block = ctx.enter_context(nc.Block())

        def split3(engine, link, b, n, src, done):
            to = slice(b, b + n)
            link(engine.tensor_copy(R3[:, to, 0, :], src))
            link(engine.tensor_tensor(rd[:, to, 0, :], src, R3[:, to, 0, :], ALU.subtract))
            link(engine.tensor_copy(R3[:, to, 1, :], rd[:, to, 0, :]))
            link(engine.tensor_tensor(rd[:, to, 1, :], rd[:, to, 0, :], R3[:, to, 1, :], ALU.subtract))
            engine.tensor_copy(R3[:, to, 2, :], rd[:, to, 1, :]).then_inc(done, 1)

        def add_residual(engine, queue, p, h):
            queue.wait_ge(s["vv"], 2 * p + h + 1)
            queue.wait_ge(s["tbeta"], p + 1)
            cols = slice(h * HALF, (h + 1) * HALF)
            engine.tensor_tensor(OUT[:, p, cols], V[:, p, cols], T[:, p, cols], ALU.add).then_inc(s_fin[2 * p + h], 1)

        def scale_tokens(engine, queue, p):
            g, l = p // 2, p % 2
            queue.wait_ge(s["pow1"], g + 1)
            queue.wait_ge(s["ones"], 1)
            engine.tensor_tensor(
                UT[:, p, :, 1:P + 1].rearrange("p j (b c) -> p j b c", b=2),
                XT[:, p, :].rearrange("p (j b c) -> p j b c", b=2, c=C),
                rt1[:, g, l * G2:(l + 1) * G2].rearrange("p (j b) -> p j b", b=2).unsqueeze(3)
                .broadcast_to([P, CH, 2, C]), ALU.mult).then_inc(s_ut[p], 1)

        @block.sync
        def _(sp):
            for p in range(NP):
                sp.dma_start(XT[:, p, :], x_tok[:, p, :]).then_inc(s_xt[p], 16)
            for p in range(NP):
                sp.dma_start(X[:, p, :], x_cha[:, p, :]).then_inc(s_x[p], 16)
            for p in range(NP):
                for half, src, done in ((0, HI, s["hi"]), (1, LO, s["lo"])):
                    sp.wait_ge(done, p + 1)
                    for b in range(2):
                        sp.dma_start(ST[half * C:(half + 1) * C, 2 * p + b, :],
                                     src[b * C:(b + 1) * C, p, :]).then_inc(s_st[p], 16)
            for p in range(NP):
                for h in range(2):
                    cols = slice(h * HALF, (h + 1) * HALF)
                    sp.wait_ge(s_fin[2 * p + h], 1)
                    sp.dma_start(out[:, p, cols], OUT[:, p, cols]).then_inc(s_out[p], 16)
            for p in range(NP):
                sp.wait_ge(s_out[p], 32)

        @block.scalar
        def _(act):
            act.dma_start(wsm[:, :], small).then_inc(s_wsm, 16)
            act.dma_start(cst[:, :], consts).then_inc(s_cst, 16)
            act.dma_start(w12_sb[:, :], w12).then_inc(s_w12, 16)
            act.dma_start(cstb[:, :], constb).then_inc(s_cstb, 16)

            def evac_gram(g):
                act.wait_ge(s["gram"], g + 1)
                nc.scalar.copy(Gs[:, g, :], ps_g[g]).then_inc(s["gs"], 1)

            def evac_u(p):
                act.wait_ge(s["tb"], p + 1)
                nc.scalar.copy(U[:, p, :], ut[:, :]).then_inc(s["u"], 1)

            def softmax_exp(g):
                act.wait_ge(s["sms"], g + 1)
                for l in range(2):
                    last = nc.scalar.activation(Ex[:, g, l, :], sm[:, g, l, :], ACT.Exp, bias=nmx[:, g, l:l + 1],
                                                accum_out=ssum[:, g, 0, l:l + 1])
                last.then_inc(s["exs"], 1)

            def evac_b1(g):
                act.wait_ge(s["b1"], g + 1)
                nc.scalar.copy(B1s[:, g, :, :], ps_b1[g]).then_inc(s["b1s"], 1)

            def evac_mt(g):
                act.wait_ge(s["mt"], g + 1)
                act.wait_ge(s["clear"], 1)
                for b in range(2):
                    rows = slice(b * C, (b + 1) * C)
                    last = nc.scalar.copy(MTs[rows, 2 * g:2 * g + 2, rows], ps_mt[g][rows, :, :])
                last.then_inc(s["mts"], 1)

            def square_t(p):
                act.wait_ge(s["t"], 2 * p + 2)
                if p >= 2:
                    act.wait_ge(s["row"], p - 1)
                nc.scalar.activation(SQ[:, p % 2, :], T[:, p, :], ACT.Square).then_inc(s["sq"], 1)

            def evac_rows(p):
                act.wait_ge(s["row"], p + 1)
                if p >= 2:
                    act.wait_ge(s["mom"], p - 1)
                nc.scalar.copy(RW[:, p % 2, :], moment_bank[p % 2][:, :]).then_inc(s["rw"], 1)

            def round_hi(p):
                act.wait_ge(s["uf"], p + 1)
                nc.scalar.copy(HI[:, p, :], UF[:, p, :]).then_inc(s["hi"], 1)

            act.wait_ge(s["wcp"], 1)
            nc.scalar.mul(wTc[:, WQ], pS[:, 0:C], D ** -0.5)
            nc.scalar.copy(wTc[:, C:3 * C + E], pS[:, C:3 * C + E])
            nc.scalar.mul(bqs[:, :], w("bq"), D ** -0.5)
            nc.scalar.copy(b2c[:, :], pS[:, 260:260 + E])
            nc.scalar.copy(wvc[:, :], pS[:, 300:300 + C]).then_inc(s["wcv"], 1)
            act.wait_ge(s["w1p"], 1)
            nc.scalar.mul(w1hl[:, :, 0, :], pC[:, :].rearrange("p (e f) -> p e f", e=E), S_W).then_inc(s["w1h"], 1)
            evac_gram(0)
            evac_u(0)
            evac_u(1)
            softmax_exp(0)
            evac_b1(0)
            evac_mt(0)
            evac_u(2)
            evac_gram(1)
            square_t(0)
            evac_u(3)
            act.wait_ge(s["w2p"], 1)
            nc.scalar.copy(w2c[:, :], ps_w2).then_inc(s["w2v"], 1)
            softmax_exp(1)
            evac_rows(0)
            evac_b1(1)
            square_t(1)
            evac_mt(1)
            evac_rows(1)
            square_t(2)
            square_t(3)
            evac_rows(2)
            evac_rows(3)
            for p in range(NP):
                round_hi(p)
            for n, src, dst in ((1, rout[:, 1, :], rout[:, 2, :]), (2, rx[:, 0, :], rx[:, 1, :]),
                                (3, rsm[:, 6, :], rsm[:, 7, :])):
                act.wait_ge(s[f"rx{n}"], 1)
                nc.scalar.activation(dst, src, ACT.Exp).then_inc(s[f"rexp{n}"], 1)
            nc.scalar.activation(gtab[:, :], w("bout"), ACT.Gelu)

            def gelu(p, k, b):
                step = TOP * p + k
                act.wait_ge(s["mm1"], 2 * step + b + 1)
                if step >= 2:
                    act.wait_ge(s["mm2"], step - 1)
                nc.scalar.activation(H[:, step % 2, b, :], h_ps[b][:, :], ACT.Gelu,
                                     bias=b1g[:, p % 2, b, k:k + 1],
                                     scale=1.0 / (S_U * S_W)).then_inc(s["gelu"], 1)

            def square_z(p):
                act.wait_ge(s["mm2"], TOP * (p + 1))
                act.wait_ge(s["c2d"], p + 1)
                if p >= 2:
                    act.wait_ge(s["row3"], p - 1)
                for n, h in enumerate((1, 0)):
                    if n:
                        act.wait_ge(s["zs"], 2 * p + 1)
                    cols = slice(h * HALF, (h + 1) * HALF)
                    nc.scalar.activation(SQ[:, p % 2, cols], y_ps[:, cols], ACT.Square,
                                         bias=c2[:, p:p + 1]).then_inc(s["sq3"], 1)

            def evac_rows3(p):
                act.wait_ge(s["row3"], p + 1)
                if p >= 2:
                    act.wait_ge(s["mom3"], p - 1)
                nc.scalar.copy(RW[:, p % 2, 0:HALF // 2], pM[:, 0:HALF // 2]).then_inc(s["rw3"], 1)

            def add_beta(p):
                nc.scalar.activation(T[:, p, :], T[:, p, :], ACT.Identity, bias=w("beta")).then_inc(s["tbeta"], 1)

            for step in range(TOP * NP):
                p, k = step // TOP, step % TOP
                if k == 1 and p >= 1:
                    square_z(p - 1)
                act.wait_ge(s["g1"], 2 * (step + 1))
                gelu(p, k, 0)
                if k == 1 and p >= 1:
                    evac_rows3(p - 1)
                gelu(p, k, 1)
                if k == 0:
                    add_beta(p)
            square_z(NP - 1)
            evac_rows3(NP - 1)

        @block.gpsimd
        def _(pool):
            count = [0]

            def link(ins):
                count[0] += 1
                ins.then_inc(s["pool"], 1)
                pool.wait_ge(s["pool"], count[0])

            nc.gpsimd.memset(UT[:, :, :, 0:P + 2:P + 1], 1.0).then_inc(s["ones"], 1)
            nc.gpsimd.memset(MTs[:, :, :], 0.0).then_inc(s["clear"], 1)

            def scale1(p):
                scale_tokens(nc.gpsimd, pool, p)

            def low(p):
                pool.wait_ge(s["uf"], p + 1)
                pool.wait_ge(s["hi"], p + 1)
                nc.gpsimd.tensor_tensor(LO[:, p, :], UF[:, p, :], HI[:, p, :],
                                        ALU.subtract).then_inc(s["lo"], 1)

            def split_group(g):
                pool.wait_ge(s["pow2"], g + 1)
                if g >= 1:
                    pool.wait_ge(s["rt"], g)
                split3(nc.gpsimd, link, 0, 2, r2[:, 2 * g:2 * g + 2, :], s["r3"])

            def gather_w1(p):
                if p >= 2:
                    pool.wait_ge(s["mm1"], 2 * TOP * (p - 1))
                    pool.wait_ge(s["gelu"], 2 * TOP * (p - 1))
                regs = []
                for k in range(TOP):
                    for b in range(2):
                        e = nc.gpsimd.value_load(i8[0:1, 2 * p + b, k:k + 1], min_val=0, max_val=E - 1)
                        regs.append(e)
                        nc.gpsimd.tensor_copy(b1g[:, p % 2, b, k:k + 1], w("b1T")[:, bass.ds(e, 1)])
                        nc.gpsimd.tensor_copy(
                            w1g[:, p % 2, b, k, :, :].rearrange("p a f -> p (a f)").bitcast(F32),
                            w1hl[:, :, :, :].rearrange("p e a f -> p (e a f)").bitcast(F32)[:, bass.ds(e * F, F)]
                        ).then_inc(s["g1"], 1)
                return regs

            def gather_w2(p, regs):
                if p >= 2:
                    pool.wait_ge(s["mm2"], TOP * (p - 1))
                    pool.wait_ge(s["c2d"], p - 1)
                for k in range(TOP):
                    for b in range(2):
                        e, wrep = regs[2 * k + b], wk[:, 2 * p + b, k:k + 1]
                        nc.gpsimd.tensor_tensor(b2g[:, p % 2, b, k:k + 1], b2c[:, bass.ds(e, 1)], wrep, ALU.mult)
                        nc.gpsimd.tensor_tensor(w2g[:, p % 2, b, k, :], w2c[:, bass.ds(e * C, C)],
                                                wrep.broadcast_to([P, C]), ALU.mult).then_inc(s["g2"], 1)

            nc.gpsimd.memset(ones_m[:, :], 1.0).then_inc(s["onesm"], 1)
            nc.gpsimd.memset(wrbd[:, :], 0.0).then_inc(s["onesm"], 1)
            pool.wait_ge(s["onesm"], 2)
            pool.wait_ge(s["wcv"], 1)
            for b in range(2):
                rows = slice(b * C, (b + 1) * C)
                nc.gpsimd.tensor_copy(wrbd[rows, b * E:(b + 1) * E], wTc[rows, WR]).then_inc(s["wrb"], 1)
                pool.wait_ge(s["wrb"], b + 1)
            scale1(1)
            scale1(3)
            split_group(0)
            split_group(1)
            low(0)
            low(1)
            pool.wait_ge(s["w1l"], 1)
            pool.wait_ge(s["w2v"], 1)
            pool.wait_ge(s["top"], 1)
            regs = gather_w1(0)
            pool.wait_ge(s["wkd"], 1)
            gather_w2(0, regs)
            gather_w2(1, gather_w1(1))
            low(2)
            low(3)
            for p in range(NP):
                if p + 2 < NP:
                    gather_w2(p + 2, gather_w1(p + 2))
                if p == NP - 1:
                    break
                pool.wait_ge(s["pow3"], p + 1)
                if p >= 2:
                    pool.wait_ge(s["rt3"], p - 1)
                else:
                    pool.wait_ge(s["rt"], 2)
                split3(nc.gpsimd, link, p % 2, 1, r3[:, p:p + 1, :], s["s3"])
                if p >= 1:
                    add_residual(nc.gpsimd, pool, p - 1, 0)
                    add_residual(nc.gpsimd, pool, p - 1, 1)
            add_residual(nc.gpsimd, pool, NP - 2, 0)
            add_residual(nc.gpsimd, pool, NP - 2, 1)
            add_residual(nc.gpsimd, pool, NP - 1, 0)

        @block.vector
        def _(dve):
            count = [0]

            def link(ins, between=None):
                count[0] += 1
                ins.then_inc(s["dve"], 1)
                if between:
                    between()
                dve.wait_ge(s["dve"], count[0])

            def rsqrt(v, y, t, q, out, done, between=None):
                link(nc.vector.tensor_scalar(q, v.bitcast(U32), 1, None, ALU.logical_shift_right), between)
                link(nc.vector.tensor_scalar(y.bitcast(U32), q, -1.0, float(0x5F3759DF), ALU.mult, ALU.add), between)
                for n in range(3):
                    link(nc.vector.scalar_tensor_tensor(out=t, in0=y, scalar=-0.5, in1=y, op0=ALU.mult,
                                                        op1=ALU.mult), between)
                    link(nc.vector.tensor_tensor(t, t, v, ALU.mult), between)
                    to = out if n == 2 else y
                    ins = nc.vector.scalar_tensor_tensor(out=to, in0=t, scalar=1.5, in1=y, op0=ALU.add, op1=ALU.mult)
                    if n == 2:
                        ins.then_inc(done, 1)
                    else:
                        link(ins, between)

            def token_stats(i):
                p, g = i // G2, i % G2
                if g == 0:
                    dve.wait_ge(s_xt[p], 16)
                return nc.vector.bn_stats(bst[:, p // 2, i % (2 * G2), :], XT[:, p, g * C:(g + 1) * C])

            done_stats, last_stats = [0], [None]

            def more_stats():
                for _ in range(1):
                    if done_stats[0] < B * CH:
                        last_stats[0] = token_stats(done_stats[0])
                        done_stats[0] += 1

            def variance1(g, between=None):
                me, ve, mo, vo = (bst[:, g, :, i] for i in (1, 2, 4, 5))
                nc.vector.tensor_tensor(cmp1[:, g, 1, :], ve, vo, ALU.add)
                link(nc.vector.tensor_tensor(cmp1[:, g, 0, :], me, mo, ALU.subtract), between)
                link(nc.vector.tensor_tensor(cmp1[:, g, 2, :], cmp1[:, g, 0, :], cmp1[:, g, 0, :], ALU.mult), between)
                link(nc.vector.scalar_tensor_tensor(out=cmp1[:, g, 1, :], in0=cmp1[:, g, 2, :], scalar=C / 4.0,
                                                    in1=cmp1[:, g, 1, :], op0=ALU.mult, op1=ALU.add), between)
                link(nc.vector.tensor_scalar(cmp1[:, g, 3, :], cmp1[:, g, 1, :], 1.0 / C, EPS_C, ALU.mult,
                                             ALU.add), between)

            def scale1(p):
                scale_tokens(nc.vector, dve, p)

            def att_p1(g):
                dve.wait_ge(s["p1"], g + 1)
                bk = w("bk").unsqueeze(1).broadcast_to([P, 2, C])
                link(nc.vector.scalar_tensor_tensor(out=vbs[:, g, 0, :, :], in0=bk, scalar=float(N), in1=ps_vb[g],
                                                    op0=ALU.mult, op1=ALU.add))
                for l in range(2):
                    last = nc.vector.scalar_tensor_tensor(
                        out=p1s[:, g, l, :], in0=w("bk"), scalar=Gs[:, g, l * G1:l * G1 + 1], in1=ps_p1[g][:, l, :],
                        op0=ALU.mult, op1=ALU.add)
                last.then_inc(s["p1s"], 1)
                link(nc.vector.scalar_tensor_tensor(out=vbs[:, g, 1, :, :], in0=vbs[:, g, 0, :, :],
                                                    scalar=bqs[:, 0:1],
                                                    in1=cf("mask").unsqueeze(1).broadcast_to([P, 2, C]),
                                                    op0=ALU.mult, op1=ALU.add))

            def att_scores(g):
                dve.wait_ge(s["s_ps"], g + 1)
                link(nc.vector.tensor_tensor(sm[:, g, :, :], vbs[:, g, 1, :, :], ps_s[g], ALU.add))
                nc.vector.tensor_reduce(nmx[:, g, :], sm[:, g, :, :], AX_X, ALU.max, negate=True).then_inc(s["sms"], 1)

            def att_probs(g):
                dve.wait_ge(s["exs"], g + 1)
                link(nc.vector.reciprocal(ssum[:, g, 1, :], ssum[:, g, 0, :]))
                nc.vector.tensor_tensor(A[:, g, :, :], Ex[:, g, :, :],
                                        ssum[:, g, 1, :].unsqueeze(2).broadcast_to([P, 2, C]),
                                        ALU.mult).then_inc(s["a_sb"], 1)

            def att_bias(g):
                dve.wait_ge(s["mts"], g + 1)
                nc.vector.tensor_tensor(cbs[:, 2 * g:2 * g + 2], w("bout").broadcast_to([P, 2]), ps_cb[g],
                                        ALU.add).then_inc(s["cbs"], 1)

            def residual1(p, halves=(0, 1)):
                dve.wait_ge(s["cbs"], p // 2 + 1)
                dve.wait_ge(s_x[p], 16)
                for h in halves:
                    cols = slice(h * HALF, (h + 1) * HALF)
                    dve.wait_ge(s["conv"], 2 * p + h + 1)
                    nc.vector.scalar_tensor_tensor(out=T[:, p, cols], in0=cv[:, cols], scalar=cbs[:, p:p + 1],
                                                   in1=X[:, p, cols], op0=ALU.add, op1=ALU.add).then_inc(s["t"], 1)

            def read_moments(p):
                dve.wait_ge(s["mom"], p + 1)
                g, cols = p // 2, slice(p % 2 * G2, (p % 2 + 1) * G2)
                pm = moments_of(moment_bank[p % 2])
                nc.vector.tensor_scalar(by_half(cmp2[:, g, 0, cols]), pm[:, 0], 1.0 / S_U, None, ALU.mult)
                nc.vector.tensor_scalar(by_half(cmp2[:, g, 1, cols]), pm[:, 1], 1.0 / S_U ** 2, EPS_T / S_U ** 2,
                                        ALU.mult, ALU.add).then_inc(s["red2"], 1)

            def rstd2(g, between=None):
                dve.wait_ge(s["red2"], 2 * (g + 1))
                link(nc.vector.tensor_tensor(cmp2[:, g, 2, :], cmp2[:, g, 0, :], cmp2[:, g, 0, :], ALU.mult))
                link(nc.vector.tensor_tensor(cmp2[:, g, 3, :], cmp2[:, g, 1, :], cmp2[:, g, 2, :], ALU.subtract))
                if g >= 1:
                    dve.wait_ge(s["pow2"], g)
                rsqrt(cmp2[:, g, 3, :], nwt[:, 0, :], nwt[:, 1, :], seed[:, :],
                      r2[:, 2 * g:2 * g + 2, :].rearrange("p l g -> p (l g)"), s["pow2"], between)

            def rows2(g):
                dve.wait_ge(s["rt"], g + 1)
                if g >= 1:
                    dve.wait_ge(s["rb"], 2 * g)
                nc.vector.tensor_copy(RR[:, :, :].rearrange("p l n -> p (l n)"), ps_rt2).then_inc(s["rr"], 1)

            def normal2(p):
                dve.wait_ge(s["rb"], p + 1)
                nc.vector.scalar_tensor_tensor(out=UF[:, p, :], in0=T[:, p, :], scalar=1.0, in1=rb[p % 2][:, :],
                                               op0=ALU.mult, op1=ALU.mult,
                                               accum_out=su[:, p:p + 1]).then_inc(s["uf"], 1)

            for i in range(2 * G2):
                last = token_stats(i)
                done_stats[0] += 1
            link(last)
            variance1(0, more_stats)
            rsqrt(cmp1[:, 0, 3, :], nwt[:, 0, :], nwt[:, 1, :], seed[:, :], rt1[:, 0, :], s["pow1"], more_stats)
            scale1(0)
            while done_stats[0] < B * CH:
                more_stats()
            link(last_stats[0])
            variance1(1)
            rsqrt(cmp1[:, 1, 3, :], nwt[:, 0, :], nwt[:, 1, :], seed[:, :], rt1[:, 1, :], s["pow1"])
            scale1(2)
            att_p1(0)
            att_scores(0)
            dve.wait_ge(s["w1p"], 1)
            dve.wait_ge(s["w1h"], 1)
            nc.vector.scalar_tensor_tensor(out=w1hl[:, :, 1, :], in0=pC[:, :].rearrange("p (e f) -> p e f", e=E),
                                           scalar=S_W, in1=w1hl[:, :, 0, :], op0=ALU.mult,
                                           op1=ALU.subtract).then_inc(s["w1l"], 1)
            att_probs(0)
            att_bias(0)
            residual1(0)
            residual1(1, [0])
            att_p1(1)
            residual1(1, [1])
            att_scores(1)
            att_probs(1)
            read_moments(0)
            att_bias(1)
            residual1(2)
            read_moments(1)
            calls = [0]

            def residual_between():
                calls[0] += 1
                if calls[0] in (2, 5):
                    residual1(3, [calls[0] // 3])

            rstd2(0, residual_between)
            read_moments(2)
            rows2(0)
            read_moments(3)
            rstd2(1)
            normal2(0)
            normal2(1)
            rows2(1)
            normal2(2)
            normal2(3)

            def be(ap):
                return ap.rearrange("p (b e) -> p b e", e=E)

            def over_e(ap):
                return ap.unsqueeze(2).broadcast_to([P, B, E])

            dve.wait_ge(s["uf"], NP)
            dve.wait_ge(s["wrb"], 2)
            nc.vector.tensor_tensor(sw[:, :].rearrange("p (l e) -> p l e", l=NP),
                                    wrbd[:, :].unsqueeze(1).broadcast_to([P, NP, 2 * E]),
                                    su[:, :].unsqueeze(2).broadcast_to([P, NP, 2 * E]), ALU.mult).then_inc(s["sw"], 1)
            dve.wait_ge(s["lg"], 1)
            link(nc.vector.scalar_tensor_tensor(out=be(rout[:, 0, :]), in0=be(ps_lg), scalar=1.0 / (S_U * N),
                                                in1=w("br").unsqueeze(1).broadcast_to([P, B, E]),
                                                op0=ALU.mult, op1=ALU.add))
            link(nc.vector.tensor_reduce(rsm[:, 0, :], be(rout[:, 0, :]), AX_X, ALU.max))
            nc.vector.tensor_tensor(be(rout[:, 1, :]), be(rout[:, 0, :]), over_e(rsm[:, 0, :]),
                                    ALU.subtract).then_inc(s["rx1"], 1)
            dve.wait_ge(s["rexp1"], 1)
            link(nc.vector.reduce_sum(rsm[:, 1, :], be(rout[:, 2, :]), AX_X))
            link(nc.vector.reciprocal(rsm[:, 2, :], rsm[:, 1, :]))
            link(nc.vector.tensor_tensor(be(rout[:, 0, :]), be(rout[:, 2, :]), over_e(rsm[:, 2, :]), ALU.mult))
            link(nc.vector.reduce_sum(rsm[:, 3, :], rout[:, 0, :].rearrange("p (b e) -> p e b", e=E), AX_X))
            link(nc.vector.reciprocal(rsm[:, 4, :], rsm[:, 3, :]))
            link(nc.vector.tensor_scalar(rsm[:, 5, :], rsm[:, 4, :], CAPACITY / N, 1.0, ALU.mult, ALU.min))
            link(nc.vector.tensor_tensor(be(rout[:, 3, :]), be(rout[:, 0, :]),
                                         rsm[:, 5, :].unsqueeze(1).broadcast_to([P, B, E]), ALU.mult))
            for i in range(B):
                last = nc.vector.max(m8[:, i, :], rout[:, 3, i * E:(i + 1) * E])
            link(last)
            for i in range(B):
                last = nc.vector.max_index(i8[:, i, :], m8[:, i, :], rout[:, 3, i * E:(i + 1) * E])
            last.then_inc(s["top"], 1)
            nc.vector.tensor_tensor(rx[:, 0, B * E:], m8[:, :, 1], m8[:, :, 0], ALU.subtract)
            nc.vector.tensor_tensor(be(rx[:, 0, 0:B * E]), be(rout[:, 3, :]),
                                    m8[:, :, 0:1].broadcast_to([P, B, E]), ALU.subtract).then_inc(s["rx2"], 1)
            dve.wait_ge(s["rexp2"], 1)
            link(nc.vector.reduce_sum(rsm[:, 0, :], be(rx[:, 1, 0:B * E]), AX_X))
            link(nc.vector.reciprocal(rsm[:, 1, :], rsm[:, 0, :]))
            link(nc.vector.tensor_scalar(rsm[:, 2, :], rx[:, 1, B * E:], 1.0, None, ALU.subtract))
            nc.vector.tensor_tensor(rsm[:, 6, :], rsm[:, 2, :], rsm[:, 1, :], ALU.mult).then_inc(s["rx3"], 1)
            dve.wait_ge(s["rexp3"], 1)
            link(nc.vector.tensor_scalar(rsm[:, 3, :], rsm[:, 7, :], 1.0, None, ALU.add))
            link(nc.vector.reciprocal(wk[:, :, 0], rsm[:, 3, :]))
            nc.vector.tensor_tensor(wk[:, :, 1], wk[:, :, 0], rsm[:, 7, :], ALU.mult).then_inc(s["wkd"], 1)

            def bias2(p):
                dve.wait_ge(s["g2"], 2 * TOP * (p + 1))
                for b in range(2):
                    rows = slice(b * C, (b + 1) * C)
                    last = nc.vector.tensor_tensor(c2[rows, p:p + 1], b2g[rows, p % 2, b, 0:1],
                                                   b2g[rows, p % 2, b, 1:2], ALU.add)
                last.then_inc(s["c2d"], 1)
                dve.wait_ge(s["c2d"], p + 1)

            def evac_z(p):
                dve.wait_ge(s["mm2"], TOP * (p + 1))
                for h in range(2):
                    if h:
                        dve.wait_ge(s["sq3"], 2 * p + 1)
                    cols = slice(h * HALF, (h + 1) * HALF)
                    nc.vector.tensor_scalar(ZS[:, p, cols], y_ps[:, cols], c2[:, p:p + 1], w("gamma"),
                                            ALU.add, ALU.mult).then_inc(s["zs"], 1)

            def rstd3(p):
                dve.wait_ge(s["mom3"], p + 1)
                pm = moments_of(pM)
                nc.vector.tensor_scalar(by_half(v3[:, p, :]), pm[:, 0], EPS_T, None, ALU.add).then_inc(s["red3"], 1)
                dve.wait_ge(s["red3"], p + 1)
                if p == 0:
                    dve.wait_ge(s["pow2"], 2)
                else:
                    dve.wait_ge(s["pow3"], p)
                rsqrt(v3[:, p, :], nwt[:, 0, 0:G2], nwt[:, 1, 0:G2], seed[:, 0:G2], r3[:, p, :], s["pow3"])

            def rows3(p):
                dve.wait_ge(s["rt3"], p + 1)
                if p >= 2:
                    dve.wait_ge(s["rb3"], 2 * (p - 1))
                nc.vector.tensor_copy(RR[:, p % 2, :], ps_rt3).then_inc(s["rr3"], 1)

            def scale_z(p, h):
                dve.wait_ge(s["rb3"], 2 * p + h + 1)
                cols = slice(h * HALF, (h + 1) * HALF)
                nc.vector.tensor_tensor(V[:, p, cols], ZS[:, p, cols], rb3[:, :], ALU.mult).then_inc(s["vv"], 1)

            bias2(0)
            bias2(1)
            for p in range(NP):
                if p < NP - 1:
                    evac_z(p)
                if p >= 1:
                    scale_z(p - 1, 0)
                    scale_z(p - 1, 1)
                rstd3(p)
                if p == NP - 2:
                    evac_z(NP - 1)
                if p == NP - 1:
                    dve.wait_ge(s["pow3"], NP)
                    dve.wait_ge(s["rt3"], NP - 2)
                    split3(nc.vector, link, p % 2, 1, r3[:, p:p + 1, :], s["s3"])
                rows3(p)
                if p + 2 < NP:
                    bias2(p + 2)
            scale_z(NP - 1, 0)
            scale_z(NP - 1, 1)
            add_residual(nc.vector, dve, NP - 1, 1)

        @block.tensor
        def _(pe):
            mm = nc.tensor.matmul

            def half(ap, b):
                return ap[b * C:(b + 1) * C]

            def gram(p):
                g, l = p // 2, p % 2
                pe.wait_ge(s["ones"], 1)
                pe.wait_ge(s_ut[p], 1)
                for j in range(CH):
                    last = mm(ps_g[g][:, l * G1:(l + 1) * G1], UT[:, p, j, 1:P + 1], UT[:, p, j, :],
                              start=(j == 0), stop=(j == CH - 1))
                if l:
                    last.then_inc(s["gram"], 1)

            def transpose_u(p):
                pe.wait_ge(s_ut[p], 1)
                if p >= 1:
                    pe.wait_ge(s["u"], p)
                for j in range(CH):
                    last = nc.tensor.transpose(ut[:, j * P:(j + 1) * P], UT[:, p, j, 1:P + 1], cf("ident"))
                last.then_inc(s["tb"], 1)

            def att_p1(g):
                pe.wait_ge(s["gs"], g + 1)
                for l in range(2):
                    for b in range(2):
                        c0 = l * G1 + 1 + b * C
                        mm(half(ps_p1[g][:, l, :], b), half(Gs[:, g, c0:c0 + C], b), half(wTc[:, WK], b),
                           start=True, stop=True)
                        last = mm(half(ps_vb[g][:, l, :], b), half(Gs[:, g, l * G1:l * G1 + 1], b).broadcast_to([C, C]),
                                  half(wTc[:, WK], b), start=True, stop=True)
                last.then_inc(s["p1"], 1)

            def att_s(g):
                pe.wait_ge(s["p1s"], g + 1)
                for l in range(2):
                    for b in range(2):
                        last = mm(half(ps_s[g][:, l, :], b), half(wTc[:, WQ], b), half(p1s[:, g, l, :], b),
                                  start=True, stop=True)
                last.then_inc(s["s_ps"], 1)

            def att_b1(g):
                pe.wait_ge(s["a_sb"], g + 1)
                for l in range(2):
                    for b in range(2):
                        last = mm(half(ps_b1[g][:, l, :], b), half(A[:, g, l, :], b), half(w("woT"), b),
                                  start=True, stop=True)
                last.then_inc(s["b1"], 1)

            def att_mt(g):
                pe.wait_ge(s["b1s"], g + 1)
                for l in range(2):
                    for b in range(2):
                        mm(half(ps_mt[g][:, l, :], b), half(wvc[:, :], b), half(B1s[:, g, l, :], b),
                           start=True, stop=True)
                        last = mm(half(ps_cb[g][:, l:l + 1], b), half(B1s[:, g, l, :], b), half(w("bv"), b),
                                  start=True, stop=True)
                last.then_inc(s["mt"], 1)

            def conv(p):
                pe.wait_ge(s["mts"], p // 2 + 1)
                pe.wait_ge(s["u"], p + 1)
                if p == 0:
                    pe.wait_ge(s["w1l"], 1)
                for h in range(2):
                    if p >= 1:
                        pe.wait_ge(s["t"], 2 * p + h - 1)
                    cols = slice(h * HALF, (h + 1) * HALF)
                    mm(cv[:, cols], MTs[:, p, :], U[:, p, cols], start=True, stop=True).then_inc(s["conv"], 1)

            def moment_rows(bank, srcs, done):
                for k, src in enumerate(srcs):
                    for q in range(4):
                        last = mm(bank[32 * q:32 * (q + 1), k * 256:(k + 1) * 256], cf("mean2"),
                                  src[:, q * 256:(q + 1) * 256], start=True, stop=True)
                last.then_inc(done, 1)

            def moment_columns(bank, n, rw, done):
                for k in range(n):
                    last = nc.tensor.transpose(bank[:, k * P:(k + 1) * P], rw[:, k * P:(k + 1) * P], cf("ident"))
                last.then_inc(done, 1)

            def rows2(p):
                pe.wait_ge(s["t"], 2 * p + 2)
                pe.wait_ge(s["sq"], p + 1)
                if p >= 2:
                    pe.wait_ge(s["red2"], p - 1)
                moment_rows(moment_bank[p % 2], [T[:, p, :], SQ[:, p % 2, :]], s["row"])

            def columns2(p):
                pe.wait_ge(s["rw"], p + 1)
                moment_columns(moment_bank[p % 2], 4, RW[:, p % 2, :], s["mom"])

            def turn(dst, l):
                return nc.tensor.transpose(dst, R3[:, l, :, :].rearrange("p k g -> p (k g)"), cb("identb"))

            def turn2(g):
                pe.wait_ge(s["r3"], g + 1)
                pe.wait_ge(s["cbs"], 2)
                if g >= 1:
                    pe.wait_ge(s["rr"], g)
                for l in range(2):
                    last = turn(ps_rt2[:, l * P:(l + 1) * P], l)
                last.then_inc(s["rt"], 1)

            def spread(dst, j0, n, p):
                for k in range(n):
                    j = j0 + k
                    last = mm(dst[:, k * P:(k + 1) * P], cb("sel")[0:3 * G2, j * P:(j + 1) * P],
                              RR[:, p % 2, :], start=True, stop=True)
                return last

            def spread2(p):
                pe.wait_ge(s["rr"], p // 2 + 1)
                if p == 0:
                    pe.wait_ge(s["t"], 2 * NP)
                elif p == 1:
                    pe.wait_ge(s["u"], NP)
                else:
                    pe.wait_ge(s["uf"], p - 1)
                spread(rb[p % 2], 0, CH, p).then_inc(s["rb"], 1)

            def spread3(p, h):
                pe.wait_ge(s["rr3"], p + 1)
                if 2 * p + h >= 1:
                    pe.wait_ge(s["vv"], 2 * p + h)
                spread(rb3, h * CH // 2, CH // 2, p).then_inc(s["rb3"], 1)

            def centre_w2(experts):
                for e in experts:
                    last = mm(ps_w2[:, e * C:(e + 1) * C], w12_sb[C:P, e * F:(e + 1) * F], cf("cend", C, P)[:, 0:C],
                              start=True, stop=True)
                if e == E - 1:
                    last.then_inc(s["w2p"], 1)

            def keep_awake(n):
                pe.wait_ge(s["w2v"], 1)
                for _ in range(n):
                    mm(ps_w2, cb("identb"), cb("sel")[:, 0:HALF], start=True, stop=True)

            pe.wait_ge(s_wsm, 16)
            pe.wait_ge(s_cst, 16)
            mm(pS[:, 0:3 * C + E], cf("cen2"), w("wT"), start=True, stop=True)
            mm(pS[:, 260:260 + E], cf("cen2"), w("b2T"), start=True, stop=True)
            for b in range(2):
                last = mm(half(pS[:, 300:300 + C], b), half(w("wvT"), b), half(cf("cend"), b)[:, 0:C],
                          start=True, stop=True)
            last.then_inc(s["wcp"], 1)
            for _ in range(3):
                mm(pM[:, 0:480], cf("ident"), cst[:, 0:480], start=True, stop=True)
            pe.wait_ge(s_w12, 16)
            for h in range(2):
                last = mm(pC[:, h * HALF:(h + 1) * HALF], cf("cend", 0, C), w12_sb[0:C, h * HALF:(h + 1) * HALF],
                          start=True, stop=True)
            last.then_inc(s["w1p"], 1)
            pe.wait_ge(s["wcv"], 1)
            pe.wait_ge(s_cstb, 16)
            gram(0)
            gram(1)
            transpose_u(0)
            att_p1(0)
            transpose_u(1)
            att_s(0)
            gram(2)
            att_b1(0)
            transpose_u(2)
            att_mt(0)
            centre_w2(range(0, E // 2))
            conv(0)
            gram(3)
            conv(1)
            att_p1(1)
            transpose_u(3)
            centre_w2(range(E // 2, E))
            att_s(1)
            rows2(0)
            keep_awake(KA[2])
            att_b1(1)
            columns2(0)
            att_mt(1)
            rows2(1)
            keep_awake(KA[3])
            conv(2)
            columns2(1)
            conv(3)
            keep_awake(KA[5])
            rows2(2)
            keep_awake(KA[6])
            rows2(3)
            columns2(2)
            keep_awake(KA[4])
            turn2(0)
            columns2(3)
            spread2(0)
            spread2(1)
            keep_awake(KA[9])
            turn2(1)
            spread2(2)
            spread2(3)
            keep_awake(KA[11])
            pe.wait_ge(s["sw"], 1)
            pe.wait_ge(s["onesm"], 1)
            mm(ps_lg, ones_m[:, :], sw[:, :], start=True, stop=True).then_inc(s["lg"], 1)
            keep_awake(KA[12])

            def up(step):
                p, k = step // TOP, step % TOP
                if k == 0:
                    pe.wait_ge(s_st[p], 64)
                for b in range(2):
                    pe.wait_ge(s["g1"], 2 * step + b + 1)
                    if step >= 1:
                        pe.wait_ge(s["gelu"], 2 * (step - 1) + b + 1)
                    for a in range(2):
                        for h in range(2):
                            cols = slice(h * HALF, (h + 1) * HALF)
                            last = mm(h_ps[b][:, cols], w1g[:, p % 2, b, k, a, :], ST[:, 2 * p + b, cols],
                                      start=(a == 0), stop=(a == 1))
                    last.then_inc(s["mm1"], 1)

            def down(step, between=None):
                p, k = step // TOP, step % TOP
                if k == 0:
                    if p >= 1:
                        pe.wait_ge(s["zs"], 2 * p)
                        pe.wait_ge(s["sq3"], 2 * p)
                    for h in range(2):
                        cols = slice(h * HALF, (h + 1) * HALF)
                        for b in range(2):
                            mm(half(y_ps[:, cols], b), cb("cenr"), ST[:, 2 * p + b, cols], start=True, stop=False)
                pe.wait_ge(s["gelu"], 2 * (step + 1))
                pe.wait_ge(s["g2"], 2 * (step + 1))
                for h in range(2):
                    cols = slice(h * HALF, (h + 1) * HALF)
                    for b in range(2):
                        last = mm(half(y_ps[:, cols], b), w2g[:, p % 2, b, k, :], H[:, step % 2, b, cols],
                                  start=False, stop=(k == TOP - 1))
                    if h == 0 and between:
                        between()
                last.then_inc(s["mm2"], 1)

            def keep_awake_at_end(n):
                for _ in range(n):
                    mm(h_ps[0][:, 0:HALF], cb("identb"), cb("sel")[:, 0:HALF], start=True, stop=True)

            def rows3(p):
                pe.wait_ge(s["sq3"], 2 * p + 2)
                if p >= 1:
                    pe.wait_ge(s["red3"], p)
                moment_rows(pM, [SQ[:, p % 2, :]], s["row3"])

            def columns3(p):
                pe.wait_ge(s["rw3"], p + 1)
                moment_columns(pM, 2, RW[:, p % 2, :], s["mom3"])

            def turn3(p):
                pe.wait_ge(s["s3"], p + 1)
                if p >= 1:
                    pe.wait_ge(s["vv"], 2 * p)
                turn(ps_rt3, p % 2).then_inc(s["rt3"], 1)

            for step in range(TOP * NP + 4):
                q, odd = (step - 5) // TOP, step % TOP
                if step < TOP * NP:
                    up(step)
                if step > TOP * NP and odd and q + 1 < NP:
                    rows3(q + 1)
                if odd and q >= 0:
                    spread3(q, 0)
                if step < TOP * NP and odd and q + 1 >= 0:
                    rows3(q + 1)
                def between():
                    if odd and q >= 0:
                        spread3(q, 1)
                    if odd and 0 <= q + 1 < NP:
                        columns3(q + 1)

                if 1 <= step <= TOP * NP:
                    down(step - 1, between)
                else:
                    between()
                if not odd and 0 <= (step - 4) // TOP < NP:
                    if step > TOP * NP:
                        keep_awake_at_end(KA[14])
                    turn3((step - 4) // TOP)
                if step == TOP * NP:
                    keep_awake_at_end(KA[13])


def kernel(x, L0_conv_Wqkv, L0_conv_bqkv, L0_conv_Wout, L0_conv_bout, L0_ffn_Wr, L0_ffn_br, L0_ffn_W1, L0_ffn_b1,
           L0_ffn_W2, L0_ffn_b2, L0_ffn_gamma, L0_ffn_beta):
    import ml_dtypes
    import numpy as np
    import concourse.bacc as bacc
    from concourse.bass_utils import run_bass_kernel_spmd

    def twice(a):
        a = np.asarray(a)
        return np.concatenate([a, a], axis=0)

    def rows(a):
        return np.broadcast_to(np.asarray(a)[None, :], (P, a.shape[0]))

    wqkv, bqkv, wout = np.asarray(L0_conv_Wqkv), np.asarray(L0_conv_bqkv), np.asarray(L0_conv_Wout)
    parts = {
        "wT": twice(np.concatenate([wqkv.T, np.asarray(L0_ffn_Wr)], axis=1)),
        "wvT": twice(wqkv[2 * C:].T), "woT": twice(wout.T.reshape(D, HEADS, C).transpose(1, 0, 2).reshape(C, C)), "bk": rows(bqkv[C:2 * C]),
        "b2T": twice(np.asarray(L0_ffn_b2).T), "b1T": np.asarray(L0_ffn_b1).T, "br": rows(L0_ffn_br),
        "bq": twice(bqkv[:C, None]), "bv": twice(bqkv[2 * C:, None]),
        "bout": twice(np.asarray(L0_conv_bout)[:, None]), "gamma": twice(np.asarray(L0_ffn_gamma)[:, None]),
        "beta": twice(np.asarray(L0_ffn_beta)[:, None]),
    }
    small = np.ascontiguousarray(np.concatenate([parts[n] for n, _ in _COLS], axis=1))
    w12 = np.ascontiguousarray(np.concatenate(
        [np.asarray(L0_ffn_W1).transpose(1, 0, 2).reshape(C, E * F),
         np.asarray(L0_ffn_W2).transpose(2, 0, 1).reshape(C, E * F)], axis=0))
    x_tok = np.ascontiguousarray(np.asarray(x).reshape(NP, 2, C, CH, P).transpose(4, 0, 3, 1, 2).reshape(P, NP, N))
    x_cha = np.ascontiguousarray(np.asarray(x).reshape(NP, P, N).transpose(1, 0, 2))

    eye = np.eye(C, dtype=np.float32)
    cen = eye - np.float32(1.0 / C)
    zero = np.zeros((C, C), np.float32)
    head = np.arange(P)[:, None] % C // D
    cons = {
        "ident": np.eye(P, dtype=np.float32), "cen2": np.block([[cen, zero], [zero, cen]]),
        "cend": np.block([[cen, cen], [cen, cen]]),
        "mean2": (np.arange(P)[:, None] // C == np.arange(32)[None, :]).astype(np.float32) / np.float32(C),
        "mask": np.where(head == np.arange(C)[None, :] // D, 0.0, -1e30).astype(np.float32),
    }
    consts = np.ascontiguousarray(np.concatenate([cons[n] for n, _ in _CONS], axis=1))
    sel = np.zeros((P, CH, P), np.float32)
    for k in range(3):
        for j in range(CH):
            for b in range(2):
                sel[k * G2 + 2 * j + b, j, b * C:(b + 1) * C] = 1.0
    conb = {"sel": sel.reshape(P, CH * P), "identb": np.eye(P, dtype=np.float32),
            "cenr": np.concatenate([cen, cen], axis=0) / np.float32(S_U)}
    constb = np.ascontiguousarray(np.concatenate([conb[n] for n, _ in _CONB], axis=1).astype(ml_dtypes.bfloat16))

    nc = bacc.Bacc("TRN2", target_bir_lowering=False, num_devices=1)
    arrays = {"x_tok_dram": x_tok, "x_cha_dram": x_cha, "small_dram": small, "w12_dram": w12, "consts_dram": consts, "constb_dram": constb}
    args = [nc.dram_tensor(n, a.shape, mybir.dt.from_np(a.dtype), kind="ExternalInput").ap()
            for n, a in arrays.items()]
    args.append(nc.dram_tensor("out_dram", (P, NP, N), F32, kind="ExternalOutput").ap())
    build_program(nc, *args)
    r = run_bass_kernel_spmd(nc, [arrays], core_ids=[0])
    got = np.asarray(r.results[0]["out_dram"])
    return np.ascontiguousarray(got.transpose(1, 0, 2)).reshape(B, C, 32, 32)
```

```python
from contextlib import ExitStack

import concourse.bass as bass
from concourse import mybir
from concourse.alu_op_type import AluOpType as ALU

F32 = mybir.dt.float32
F16 = mybir.dt.float16
BF16 = mybir.dt.bfloat16
U32 = mybir.dt.uint32
ACT = mybir.ActivationFunctionType
AX_X = mybir.AxisListType.X

P = 128
B, C, N = 8, 64, 1024
NP = B // 2
CH = N // P
G2 = 2 * CH
HALF = N // 2
HEADS = 8
D = C // HEADS
E, F = 8, 128
TOP = 2
RSQRT = (8 / 3) ** 2
CAPACITY = float(-(-(B * N * 5 // 4) // E))
EPS_C, EPS_T = 1e-6, 1e-5
S_U, S_W = 16.0, 64.0

_COLS = [("wT", 3 * C + E), ("wvT", C), ("woT", C), ("bk", C), ("b2T", E), ("b1T", E), ("br", E),
         ("bq", 1), ("bv", 1), ("bout", 1), ("gamma", 1), ("beta", 1)]
_CONS = [("ident", P), ("cen2", P), ("cend", P), ("mean2", 32), ("mask", C)]
_CONB = [("sel", CH * P), ("identb", P), ("cenr", C)]


def offsets(cols):
    at, out = 0, {}
    for name, n in cols:
        out[name] = (at, at + n)
        at += n
    return out, at


OFF_W, W_COLS = offsets(_COLS)
OFF_C, C_COLS = offsets(_CONS)
OFF_B, B_COLS = offsets(_CONB)


def build_program(nc, x_tok, x_cha, small, w12, consts, constb, out):
    with ExitStack() as ctx:
        def sb(name, shape, dt=F32):
            return ctx.enter_context(nc.sbuf_tensor(name, shape, dt))

        def sem(name):
            return ctx.enter_context(nc.semaphore(name))

        wsm = sb("wsm", [P, W_COLS])
        cst = sb("cst", [P, C_COLS])
        cstb = sb("cstb", [P, B_COLS], BF16)
        w12_sb = sb("w12_sb", [P, E * F])
        XT = sb("XT", [P, NP, N])
        X = sb("X", [P, NP, N])
        T = sb("T", [P, NP, N])
        UT = sb("UT", [P, NP, CH, P + 2])
        U = sb("U", [P, NP, N])
        SQ = sb("SQ", [P, 2, N])
        UF = sb("UF", [P, NP, N])
        HI = sb("HI", [P, NP, N], F16)
        LO = sb("LO", [P, NP, N], F16)
        ST = sb("ST", [P, B, N], F16)
        H = sb("H", [P, 2, 2, N])
        ZS, V, OUT = U, XT, XT
        wTc = sb("wTc", [P, 3 * C + E])
        wvc = sb("wvc", [P, C])
        bqs = sb("bqs", [P, 1])
        w1hl = sb("w1hl", [P, E, 2, F], F16)
        w2c = sb("w2c", [P, E * C])
        b2c = sb("b2c", [P, E])
        bst = sb("bst", [P, 2, 2 * G2, 6])
        cmp1 = sb("cmp1", [P, 2, 4, 2 * G2])
        rt1 = sb("rt1", [P, 2, 2 * G2])
        Gs = sb("Gs", [P, 2, 2 * (P + 2)])
        p1s = sb("p1s", [P, 2, 2, C])
        vbs = sb("vbs", [P, 2, 2, 2, C])
        sm = sb("sm", [P, 2, 2, C])
        nmx = sb("nmx", [P, 2, 2])
        Ex = sb("Ex", [P, 2, 2, C])
        ssum = sb("ssum", [P, 2, 2, 2])
        A = sb("A", [P, 2, 2, C])
        B1s = sb("B1s", [P, 2, 2, C])
        MTs = sb("MTs", [P, NP, P])
        cbs = sb("cbs", [P, NP])
        RW = sb("RW", [P, 2, HALF])
        cmp2 = sb("cmp2", [P, 2, 4, 2 * G2])
        seed = sb("seed", [P, 2 * G2], U32)
        nwt = sb("nwt", [P, 2, 2 * G2])
        r2 = sb("r2", [P, NP, G2])
        v3 = sb("v3", [P, NP, G2])
        r3 = sb("r3", [P, NP, G2])
        rd = sb("rd", [P, 2, G2])
        R3 = sb("R3", [P, 2, 3, G2], BF16)
        RR = sb("RR", [3 * G2, 2, P], BF16)
        su = sb("su", [P, NP])
        wrbd = sb("wrbd", [P, 2 * E])
        sw = sb("sw", [P, B * E])
        ones_m = sb("ones_m", [P, P])
        rout = sb("rout", [P, 4, B * E])
        rx = sb("rx", [P, 2, (E + 1) * B])
        rsm = sb("rsm", [P, 8, B])
        m8 = sb("m8", [P, B, 8])
        i8 = sb("i8", [P, B, 8], U32)
        wk = sb("wk", [P, B, TOP])
        w2g = sb("w2g", [P, 2, 2, TOP, C])
        b1g = sb("b1g", [P, 2, 2, TOP])
        b2g = sb("b2g", [P, 2, 2, TOP])
        c2 = sb("c2", [P, NP])
        gtab = sb("gtab", [P, 1])

        def w(name, p0=0, p1=P):
            a, b = OFF_W[name]
            return wsm[p0:p1, a:b]

        def cf(name, p0=0, p1=P):
            a, b = OFF_C[name]
            return cst[p0:p1, a:b]

        def cb(name, p0=0, p1=P):
            a, b = OFF_B[name]
            return cstb[p0:p1, a:b]

        def moments_of(bank):
            return bank.rearrange("p (s h q r) -> p s h q r", s=2, h=2, r=32)[:, :, :, :, 0:2]

        def by_half(ap):
            return ap.rearrange("p (q h b) -> p h q b", h=2, b=2)

        WQ, WK, WR = slice(0, C), slice(C, 2 * C), slice(3 * C, 3 * C + E)

        pA = ctx.enter_context(nc.psum_tensor("pA", [P, N], F32))
        pB = ctx.enter_context(nc.psum_tensor("pB", [P, N], F32))
        pC = ctx.enter_context(nc.psum_tensor("pC", [P, N], F32))
        pS = ctx.enter_context(nc.psum_tensor("pS", [P, HALF], F32))
        pM = ctx.enter_context(nc.psum_tensor("pM", [P, HALF], F32))
        ut, cv = pA, pC
        rb = [pC, pA]
        h_ps, y_ps = [pA, pB], pC
        G1 = P + 2
        small_bank = [pS, pB]

        def pair_view(ap):
            return ap.rearrange("p (l c) -> p l c", l=2)

        ps_g = [q[:, 0:2 * G1] for q in small_bank]
        ps_p1 = [pair_view(q[:, 260:388]) for q in small_bank]
        ps_vb = [pair_view(q[:, 0:128]) for q in small_bank]
        ps_s = [pair_view(q[:, 128:256]) for q in small_bank]
        ps_b1, ps_mt, ps_cb = ps_p1, ps_vb, [q[:, 388:390] for q in small_bank]
        moment_bank = [pM, pS]
        ps_w2 = pB[:, HALF:N]
        ps_rt2 = pB[0:3 * G2, 0:P].bitcast(BF16)
        ps_rt3 = [q[0:3 * G2, 0:P // 2].bitcast(BF16) for q in (pS, pS, pS, pB)]
        rb3 = [[pS[:, :], pS[:, :]]] * (NP - 1) + [[pB[:, HALF:N], pA[:, HALF:N]]]
        ps_lg = pS[:, 0:B * E]

        s_cst, s_cstb, s_wsm, s_w12 = sem("s_cst"), sem("s_cstb"), sem("s_wsm"), sem("s_w12")
        s_xt = [sem(f"s_xt{p}") for p in range(NP)]
        s_xt_first = sem("s_xt_first")
        s_x = [sem(f"s_x{p}") for p in range(NP)]
        s_ut = [sem(f"s_ut{p}") for p in range(NP)]
        s_fin = [sem(f"s_fin{i}") for i in range(2 * NP)]
        s_sq = [sem(f"s_squared{p}") for p in range(NP)]
        s_st = [sem(f"s_st{p}") for p in range(NP)]
        s_out = [sem(f"s_out{p}") for p in range(NP)]
        names = ("ones clear onesm wrb sw wcp wcv gram gs tb u p1 p1s s_ps sms exs a_sb b1 b1s mt mts cbs conv t "
                 "row rw mom pow1 pow2 red2 r3 rt rr rb uf hi lo w1p w1h w1l w2p w2v lg rexp1 rexp2 "
                 "half_tanh rx1 rx2 rx3 wkd top "
                 "g1 g2 c2d mm1 gelu mm2 zs sq3 row3 rw3 mom3 red3 pow3 s3 rt3 rr3 rb3 vv tbeta dve pool").split()
        s = {n: sem("s_" + n) for n in names}

        block = ctx.enter_context(nc.Block())

        def split3(engine, link, b, n, src, done):
            to = slice(b, b + n)
            link(engine.tensor_copy(R3[:, to, 0, :], src))
            engine.tensor_tensor(rd[:, to, :], src, R3[:, to, 0, :], ALU.subtract)
            link(engine.tensor_tensor(R3[:, to, 1, :], src, R3[:, to, 0, :], ALU.subtract))
            engine.tensor_tensor(R3[:, to, 2, :], rd[:, to, :], R3[:, to, 1, :], ALU.subtract).then_inc(done, 1)

        def add_residual(engine, queue, p, h):
            queue.wait_ge(s["vv"], 2 * p + h + 1)
            queue.wait_ge(s["tbeta"], p + 1)
            cols = slice(h * HALF, (h + 1) * HALF)
            engine.tensor_tensor(OUT[:, p, cols], V[:, p, cols], T[:, p, cols], ALU.add).then_inc(s_fin[2 * p + h], 1)

        def scale_tokens(engine, queue, p):
            g, l = p // 2, p % 2
            queue.wait_ge(s["pow1"], g + 1)
            queue.wait_ge(s["ones"], 1)
            engine.tensor_tensor(
                UT[:, p, :, 1:P + 1].rearrange("p j (b c) -> p j b c", b=2),
                XT[:, p, :].rearrange("p (j b c) -> p j b c", b=2, c=C),
                rt1[:, g, l * G2:(l + 1) * G2].rearrange("p (j b) -> p j b", b=2).unsqueeze(3)
                .broadcast_to([P, CH, 2, C]), ALU.mult).then_inc(s_ut[p], 1)

        @block.sync
        def _(sp):
            sp.dma_start(XT[:, 0, 0:HALF], x_tok[:, 0, 0:HALF]).then_inc(s_xt_first, 16)
            sp.dma_start(XT[:, 1, :], x_tok[:, 1, :]).then_inc(s_xt[1], 16)
            for p in range(2, NP):
                sp.dma_start(XT[:, p, :], x_tok[:, p, :]).then_inc(s_xt[p], 16)
            sp.dma_start(wsm[:, :], small).then_inc(s_wsm, 16)
            for p in range(NP):
                sp.dma_start(X[:, p, :], x_cha[:, p, :]).then_inc(s_x[p], 16)
            for p in range(NP):
                for half, src, done in ((0, HI, s["hi"]), (1, LO, s["lo"])):
                    sp.wait_ge(done, p + 1)
                    for b in range(2):
                        sp.dma_start(ST[half * C:(half + 1) * C, 2 * p + b, :],
                                     src[b * C:(b + 1) * C, p, :]).then_inc(s_st[p], 16)
            for p in range(NP):
                for h in range(2):
                    cols = slice(h * HALF, (h + 1) * HALF)
                    sp.wait_ge(s_fin[2 * p + h], 1)
                    sp.dma_start(out[:, p, cols], OUT[:, p, cols]).then_inc(s_out[p], 16)
            for p in range(NP):
                sp.wait_ge(s_out[p], 32)

        @block.scalar
        def _(act):
            act.dma_start(XT[:, 0, HALF:N], x_tok[:, 0, HALF:N]).then_inc(s_xt[0], 16)
            act.dma_start(cst[:, :], consts).then_inc(s_cst, 16)
            act.dma_start(w12_sb[:, :], w12).then_inc(s_w12, 16)
            act.dma_start(cstb[:, :], constb).then_inc(s_cstb, 16)

            def evac_gram(g):
                act.wait_ge(s["gram"], g + 1)
                nc.scalar.copy(Gs[:, g, :], ps_g[g]).then_inc(s["gs"], 1)

            def evac_u(p):
                act.wait_ge(s["tb"], p + 1)
                nc.scalar.copy(U[:, p, :], ut[:, :]).then_inc(s["u"], 1)

            def softmax_exp(g):
                act.wait_ge(s["sms"], g + 1)
                for l in range(2):
                    last = nc.scalar.activation(Ex[:, g, l, :], sm[:, g, l, :], ACT.Exp, bias=nmx[:, g, l:l + 1],
                                                accum_out=ssum[:, g, 0, l:l + 1])
                last.then_inc(s["exs"], 1)

            def evac_b1(g):
                act.wait_ge(s["b1"], g + 1)
                nc.scalar.copy(B1s[:, g, :, :], ps_b1[g]).then_inc(s["b1s"], 1)

            def evac_mt(g):
                act.wait_ge(s["mt"], g + 1)
                act.wait_ge(s["clear"], 1)
                for b in range(2):
                    rows = slice(b * C, (b + 1) * C)
                    last = nc.scalar.copy(MTs[rows, 2 * g:2 * g + 2, rows], ps_mt[g][rows, :, :])
                last.then_inc(s["mts"], 1)

            def square_t(p):
                act.wait_ge(s["t"], 2 * p + 2)
                if p >= 2:
                    act.wait_ge(s["row"], p - 1)
                nc.scalar.activation(SQ[:, p % 2, :], T[:, p, :], ACT.Square).then_inc(s_sq[p], 1)

            def evac_rows(p):
                act.wait_ge(s["row"], p + 1)
                if p >= 2:
                    act.wait_ge(s["mom"], p - 1)
                nc.scalar.copy(RW[:, p % 2, :], moment_bank[p % 2][:, :]).then_inc(s["rw"], 1)

            def round_hi(p):
                act.wait_ge(s["uf"], p + 1)
                nc.scalar.copy(HI[:, p, :], UF[:, p, :]).then_inc(s["hi"], 1)

            def add_beta(p):
                nc.scalar.activation(T[:, p, :], T[:, p, :], ACT.Identity, bias=w("beta")).then_inc(s["tbeta"], 1)

            act.wait_ge(s["w1p"], 1)
            nc.scalar.mul(w1hl[:, :, 0, :], pC[:, :].rearrange("p (e f) -> p e f", e=E), S_W).then_inc(s["w1h"], 1)
            act.wait_ge(s["wcp"], 1)
            nc.scalar.mul(wTc[:, WQ], pS[:, 0:C], D ** -0.5)
            nc.scalar.copy(wTc[:, C:3 * C + E], pS[:, C:3 * C + E])
            nc.scalar.mul(bqs[:, :], w("bq"), D ** -0.5)
            nc.scalar.copy(b2c[:, :], pS[:, 260:260 + E])
            nc.scalar.copy(wvc[:, :], pS[:, 300:300 + C]).then_inc(s["wcv"], 1)
            evac_gram(0)
            evac_u(0)
            evac_u(1)
            softmax_exp(0)
            evac_b1(0)
            evac_mt(0)
            evac_u(2)
            evac_gram(1)
            square_t(0)
            evac_u(3)
            softmax_exp(1)
            evac_rows(0)
            evac_b1(1)
            evac_rows(1)
            evac_mt(1)
            square_t(2)
            square_t(3)
            evac_rows(2)
            evac_rows(3)
            act.wait_ge(s["w2p"], 2)
            nc.scalar.copy(w2c[:, :], ps_w2).then_inc(s["w2v"], 1)
            for p in range(NP):
                round_hi(p)
            for n, src, dst in ((1, rout[:, 1, :], rout[:, 2, :]), (2, rx[:, 0, :], rx[:, 1, :])):
                act.wait_ge(s[f"rx{n}"], 1)
                nc.scalar.activation(dst, src, ACT.Exp).then_inc(s[f"rexp{n}"], 1)
                if n == 1:
                    add_beta(0)
                    add_beta(1)
            nc.scalar.activation(gtab[:, :], w("bout"), ACT.Gelu)
            act.wait_ge(s["rx3"], 1)
            nc.scalar.activation(rsm[:, 7, :], rsm[:, 6, :], ACT.Tanh, scale=0.5).then_inc(s["half_tanh"], 1)

            def gelu(p, k, b):
                step = TOP * p + k
                act.wait_ge(s["mm1"], 2 * step + b + 1)
                if step >= 2:
                    act.wait_ge(s["mm2"], step - 1)
                nc.scalar.activation(H[:, step % 2, b, :], h_ps[b][:, :], ACT.Gelu,
                                     bias=b1g[:, p % 2, b, k:k + 1],
                                     scale=1.0 / (S_U * S_W)).then_inc(s["gelu"], 1)

            def square_z(p):
                act.wait_ge(s["mm2"], TOP * (p + 1))
                act.wait_ge(s["c2d"], p + 1)
                if p >= 2:
                    act.wait_ge(s["row3"], p - 1)
                for n, h in enumerate((1, 0)):
                    if n:
                        act.wait_ge(s["zs"], 2 * p + 1)
                    cols = slice(h * HALF, (h + 1) * HALF)
                    nc.scalar.activation(SQ[:, p % 2, cols], y_ps[:, cols], ACT.Square,
                                         bias=c2[:, p:p + 1]).then_inc(s["sq3"], 1)

            def evac_rows3(p):
                act.wait_ge(s["row3"], p + 1)
                if p >= 2:
                    act.wait_ge(s["mom3"], p - 1)
                nc.scalar.copy(RW[:, p % 2, 0:HALF // 2], pM[:, 0:HALF // 2]).then_inc(s["rw3"], 1)

            for step in range(TOP * NP):
                p, k = step // TOP, step % TOP
                if k == 1 and p >= 1:
                    square_z(p - 1)
                act.wait_ge(s["g1"], 2 * (step + 1))
                gelu(p, k, 0)
                if k == 1 and p >= 1:
                    evac_rows3(p - 1)
                gelu(p, k, 1)
                if k == 0 and p >= 2:
                    add_beta(p)
            square_z(NP - 1)
            evac_rows3(NP - 1)

        @block.gpsimd
        def _(pool):
            count = [0]

            def link(ins):
                count[0] += 1
                ins.then_inc(s["pool"], 1)
                pool.wait_ge(s["pool"], count[0])

            nc.gpsimd.memset(UT[:, :, :, 0:P + 2:P + 1], 1.0).then_inc(s["ones"], 1)
            nc.gpsimd.memset(MTs[:, :, :], 0.0).then_inc(s["clear"], 1)

            def scale1(p):
                scale_tokens(nc.gpsimd, pool, p)

            def low(p):
                pool.wait_ge(s["uf"], p + 1)
                pool.wait_ge(s["hi"], p + 1)
                nc.gpsimd.tensor_tensor(LO[:, p, :], UF[:, p, :], HI[:, p, :],
                                        ALU.subtract).then_inc(s["lo"], 1)

            def split_group(g):
                pool.wait_ge(s["pow2"], g + 1)
                if g >= 1:
                    pool.wait_ge(s["rt"], g)
                split3(nc.gpsimd, link, 0, 2, r2[:, 2 * g:2 * g + 2, :], s["r3"])

            def gather_b1(p):
                if p >= 2:
                    pool.wait_ge(s["gelu"], 2 * TOP * (p - 1))
                regs = []
                if p <= 1:
                    pool.wait_ge(s["top"], 1 + p)
                for k in range(TOP):
                    for b in range(2):
                        e = nc.gpsimd.value_load(i8[0:1, 2 * p + b, k:k + 1], min_val=0, max_val=E - 1)
                        regs.append(e)
                        nc.gpsimd.tensor_copy(b1g[:, p % 2, b, k:k + 1],
                                              w("b1T")[:, bass.ds(e, 1)]).then_inc(s["g1"], 1)
                return regs

            def gather_w2(p, regs):
                if p >= 2:
                    pool.wait_ge(s["mm2"], TOP * (p - 1))
                    pool.wait_ge(s["c2d"], p - 1)
                for k in range(TOP):
                    for b in range(2):
                        e, wrep = regs[2 * k + b], wk[:, 2 * p + b, k:k + 1]
                        nc.gpsimd.tensor_tensor(b2g[:, p % 2, b, k:k + 1], b2c[:, bass.ds(e, 1)], wrep, ALU.mult)
                        nc.gpsimd.tensor_tensor(w2g[:, p % 2, b, k, :], w2c[:, bass.ds(e * C, C)],
                                                wrep.broadcast_to([P, C]), ALU.mult).then_inc(s["g2"], 1)

            nc.gpsimd.memset(ones_m[:, :], 1.0).then_inc(s["onesm"], 1)
            nc.gpsimd.memset(wrbd[:, :], 0.0).then_inc(s["onesm"], 1)
            pool.wait_ge(s["onesm"], 2)
            scale1(1)
            scale1(2)
            scale1(3)
            pool.wait_ge(s["wcv"], 1)
            for b in range(2):
                rows = slice(b * C, (b + 1) * C)
                nc.gpsimd.tensor_copy(wrbd[rows, b * E:(b + 1) * E], wTc[rows, WR]).then_inc(s["wrb"], 1)
                pool.wait_ge(s["wrb"], b + 1)
            pool.wait_ge(s["t"], 4)
            nc.gpsimd.tensor_tensor(SQ[:, 1, :], T[:, 1, :], T[:, 1, :], ALU.mult).then_inc(s_sq[1], 1)
            split_group(0)
            split_group(1)
            low(0)
            low(1)
            pool.wait_ge(s["w1l"], 1)
            pool.wait_ge(s["w2v"], 1)
            regs = gather_b1(0)
            pool.wait_ge(s["wkd"], 1)
            gather_w2(0, regs)
            gather_w2(1, gather_b1(1))
            low(2)
            low(3)
            for p in range(NP):
                if p + 2 < NP:
                    gather_w2(p + 2, gather_b1(p + 2))
                if p == NP - 1:
                    break
                pool.wait_ge(s["pow3"], p + 1)
                if p >= 2:
                    pool.wait_ge(s["rt3"], p - 1)
                else:
                    pool.wait_ge(s["rt"], 2)
                split3(nc.gpsimd, link, p % 2, 1, r3[:, p:p + 1, :], s["s3"])
                if p >= 1:
                    add_residual(nc.gpsimd, pool, p - 1, 0)
                    add_residual(nc.gpsimd, pool, p - 1, 1)
            add_residual(nc.gpsimd, pool, NP - 2, 0)
            add_residual(nc.gpsimd, pool, NP - 2, 1)
            add_residual(nc.gpsimd, pool, NP - 1, 0)

        @block.vector
        def _(dve):
            count = [0]

            def link(ins, between=None):
                count[0] += 1
                ins.then_inc(s["dve"], 1)
                if between:
                    between()
                dve.wait_ge(s["dve"], count[0])

            def rsqrt(v, y, t, q, out, done, between=None):
                link(nc.vector.tensor_scalar(q, v.bitcast(U32), 1, None, ALU.logical_shift_right), between)
                link(nc.vector.tensor_scalar(y.bitcast(U32), q, -1.0, float(0x5F3759DF), ALU.mult, ALU.add), between)
                link(nc.vector.tensor_tensor(t, y, y, ALU.mult), between)
                link(nc.vector.tensor_tensor(t, t, v, ALU.mult), between)
                link(nc.vector.scalar_tensor_tensor(out=t, in0=t, scalar=-10.0 / 3.0, in1=t, op0=ALU.add,
                                                    op1=ALU.mult), between)
                link(nc.vector.scalar_tensor_tensor(out=y, in0=t, scalar=5.0, in1=y, op0=ALU.add, op1=ALU.mult), between)
                link(nc.vector.scalar_tensor_tensor(out=t, in0=y, scalar=-0.5 * (3 / 8) ** 2, in1=y, op0=ALU.mult,
                                                    op1=ALU.mult), between)
                link(nc.vector.tensor_tensor(t, t, v, ALU.mult), between)
                nc.vector.scalar_tensor_tensor(out=out, in0=t, scalar=1.5, in1=y, op0=ALU.add,
                                               op1=ALU.mult).then_inc(done, 1)

            def token_stats(i):
                p, g = i // G2, i % G2
                if i == 0:
                    dve.wait_ge(s_xt_first, 16)
                if i == G2 // 2 or (p and g == 0):
                    dve.wait_ge(s_xt[p], 16)
                return nc.vector.bn_stats(bst[:, p // 2, i % (2 * G2), :], XT[:, p, g * C:(g + 1) * C])

            done_stats, last_stats = [0], [None]

            def more_stats():
                for _ in range(1):
                    if done_stats[0] < B * CH:
                        last_stats[0] = token_stats(done_stats[0])
                        done_stats[0] += 1

            def variance1(g, between=None):
                me, ve, mo, vo = (bst[:, g, :, i] for i in (1, 2, 4, 5))
                nc.vector.tensor_tensor(cmp1[:, g, 1, :], ve, vo, ALU.add)
                link(nc.vector.tensor_tensor(cmp1[:, g, 0, :], me, mo, ALU.subtract), between)
                link(nc.vector.tensor_tensor(cmp1[:, g, 2, :], cmp1[:, g, 0, :], cmp1[:, g, 0, :], ALU.mult), between)
                link(nc.vector.scalar_tensor_tensor(out=cmp1[:, g, 1, :], in0=cmp1[:, g, 2, :], scalar=C / 4.0,
                                                    in1=cmp1[:, g, 1, :], op0=ALU.mult, op1=ALU.add), between)
                link(nc.vector.tensor_scalar(cmp1[:, g, 3, :], cmp1[:, g, 1, :], RSQRT / C, RSQRT * EPS_C, ALU.mult,
                                             ALU.add), between)

            def scale1(p):
                scale_tokens(nc.vector, dve, p)

            def att_p1(g):
                dve.wait_ge(s["p1"], g + 1)
                bk = w("bk").unsqueeze(1).broadcast_to([P, 2, C])
                link(nc.vector.scalar_tensor_tensor(out=vbs[:, g, 0, :, :], in0=bk, scalar=float(N), in1=ps_vb[g],
                                                    op0=ALU.mult, op1=ALU.add))
                for l in range(2):
                    last = nc.vector.scalar_tensor_tensor(
                        out=p1s[:, g, l, :], in0=w("bk"), scalar=Gs[:, g, l * G1:l * G1 + 1], in1=ps_p1[g][:, l, :],
                        op0=ALU.mult, op1=ALU.add)
                last.then_inc(s["p1s"], 1)
                link(nc.vector.scalar_tensor_tensor(out=vbs[:, g, 1, :, :], in0=vbs[:, g, 0, :, :],
                                                    scalar=bqs[:, 0:1],
                                                    in1=cf("mask").unsqueeze(1).broadcast_to([P, 2, C]),
                                                    op0=ALU.mult, op1=ALU.add))

            def att_scores(g):
                dve.wait_ge(s["s_ps"], g + 1)
                link(nc.vector.tensor_tensor(sm[:, g, :, :], vbs[:, g, 1, :, :], ps_s[g], ALU.add))
                nc.vector.tensor_reduce(nmx[:, g, :], sm[:, g, :, :], AX_X, ALU.max, negate=True).then_inc(s["sms"], 1)

            def att_probs(g):
                dve.wait_ge(s["exs"], g + 1)
                link(nc.vector.reciprocal(ssum[:, g, 1, :], ssum[:, g, 0, :]))
                nc.vector.tensor_tensor(A[:, g, :, :], Ex[:, g, :, :],
                                        ssum[:, g, 1, :].unsqueeze(2).broadcast_to([P, 2, C]),
                                        ALU.mult).then_inc(s["a_sb"], 1)

            def att_bias(g):
                dve.wait_ge(s["mts"], g + 1)
                nc.vector.tensor_tensor(cbs[:, 2 * g:2 * g + 2], w("bout").broadcast_to([P, 2]), ps_cb[g],
                                        ALU.add).then_inc(s["cbs"], 1)

            def residual1(p, halves=(0, 1)):
                dve.wait_ge(s["cbs"], p // 2 + 1)
                dve.wait_ge(s_x[p], 16)
                for h in halves:
                    cols = slice(h * HALF, (h + 1) * HALF)
                    dve.wait_ge(s["conv"], 2 * p + h + 1)
                    nc.vector.scalar_tensor_tensor(out=T[:, p, cols], in0=cv[:, cols], scalar=cbs[:, p:p + 1],
                                                   in1=X[:, p, cols], op0=ALU.add, op1=ALU.add).then_inc(s["t"], 1)

            def read_moments(p):
                dve.wait_ge(s["mom"], p + 1)
                g, cols = p // 2, slice(p % 2 * G2, (p % 2 + 1) * G2)
                pm = moments_of(moment_bank[p % 2])
                nc.vector.tensor_scalar(by_half(cmp2[:, g, 0, cols]), pm[:, 0], RSQRT ** 0.5 / S_U, None, ALU.mult)
                nc.vector.tensor_scalar(by_half(cmp2[:, g, 1, cols]), pm[:, 1], RSQRT / S_U ** 2,
                                        RSQRT * EPS_T / S_U ** 2, ALU.mult, ALU.add).then_inc(s["red2"], 1)

            def rstd2(g, between=None):
                dve.wait_ge(s["red2"], 2 * (g + 1))
                link(nc.vector.tensor_tensor(cmp2[:, g, 2, :], cmp2[:, g, 0, :], cmp2[:, g, 0, :], ALU.mult))
                link(nc.vector.tensor_tensor(cmp2[:, g, 3, :], cmp2[:, g, 1, :], cmp2[:, g, 2, :], ALU.subtract))
                if g >= 1:
                    dve.wait_ge(s["pow2"], g)
                rsqrt(cmp2[:, g, 3, :], nwt[:, 0, :], nwt[:, 1, :], seed[:, :],
                      r2[:, 2 * g:2 * g + 2, :].rearrange("p l g -> p (l g)"), s["pow2"], between)

            def rows2(g):
                dve.wait_ge(s["rt"], g + 1)
                if g >= 1:
                    dve.wait_ge(s["rb"], 2 * g)
                nc.vector.tensor_copy(RR[:, :, :].rearrange("p l n -> p (l n)"), ps_rt2).then_inc(s["rr"], 1)

            def normal2(p):
                dve.wait_ge(s["rb"], p + 1)
                nc.vector.scalar_tensor_tensor(out=UF[:, p, :], in0=T[:, p, :], scalar=1.0, in1=rb[p % 2][:, :],
                                               op0=ALU.mult, op1=ALU.mult,
                                               accum_out=su[:, p:p + 1]).then_inc(s["uf"], 1)

            for i in range(2 * G2):
                last = token_stats(i)
                done_stats[0] += 1
            link(last)
            variance1(0, more_stats)
            rsqrt(cmp1[:, 0, 3, :], nwt[:, 0, :], nwt[:, 1, :], seed[:, :], rt1[:, 0, :], s["pow1"], more_stats)
            scale1(0)
            while done_stats[0] < B * CH:
                more_stats()
            link(last_stats[0])
            variance1(1)
            rsqrt(cmp1[:, 1, 3, :], nwt[:, 0, :], nwt[:, 1, :], seed[:, :], rt1[:, 1, :], s["pow1"])
            att_p1(0)
            att_scores(0)
            dve.wait_ge(s["w1p"], 1)
            dve.wait_ge(s["w1h"], 1)
            nc.vector.scalar_tensor_tensor(out=w1hl[:, :, 1, :], in0=pC[:, :].rearrange("p (e f) -> p e f", e=E),
                                           scalar=S_W, in1=w1hl[:, :, 0, :], op0=ALU.mult,
                                           op1=ALU.subtract).then_inc(s["w1l"], 1)
            att_probs(0)
            att_bias(0)
            residual1(0)
            residual1(1, [0])
            att_p1(1)
            residual1(1, [1])
            att_scores(1)
            att_probs(1)
            read_moments(0)
            att_bias(1)
            residual1(2)
            read_moments(1)
            calls = [0]

            def residual_between():
                calls[0] += 1
                if calls[0] in (1, 3):
                    residual1(3, [calls[0] // 2])

            rstd2(0, residual_between)
            read_moments(2)
            read_moments(3)
            calls[0] = 0

            def rows_between():
                calls[0] += 1
                if calls[0] == 1:
                    rows2(0)

            rstd2(1, rows_between)
            normal2(0)
            rows2(1)
            normal2(1)
            normal2(2)
            normal2(3)

            def be(ap):
                return ap.rearrange("p (b e) -> p b e", e=E)

            def over_e(ap):
                return ap.unsqueeze(2).broadcast_to([P, B, E])

            dve.wait_ge(s["uf"], NP)
            dve.wait_ge(s["wrb"], 2)
            nc.vector.tensor_tensor(sw[:, :].rearrange("p (l e) -> p l e", l=NP),
                                    wrbd[:, :].unsqueeze(1).broadcast_to([P, NP, 2 * E]),
                                    su[:, :].unsqueeze(2).broadcast_to([P, NP, 2 * E]), ALU.mult).then_inc(s["sw"], 1)
            dve.wait_ge(s["lg"], 1)
            link(nc.vector.scalar_tensor_tensor(out=be(rout[:, 0, :]), in0=be(ps_lg), scalar=1.0 / (S_U * N),
                                                in1=w("br").unsqueeze(1).broadcast_to([P, B, E]),
                                                op0=ALU.mult, op1=ALU.add))
            link(nc.vector.tensor_reduce(rsm[:, 0, :], be(rout[:, 0, :]), AX_X, ALU.max))
            nc.vector.tensor_tensor(be(rout[:, 1, :]), be(rout[:, 0, :]), over_e(rsm[:, 0, :]),
                                    ALU.subtract).then_inc(s["rx1"], 1)
            dve.wait_ge(s["rexp1"], 1)
            link(nc.vector.reduce_sum(rsm[:, 1, :], be(rout[:, 2, :]), AX_X))
            link(nc.vector.reciprocal(rsm[:, 2, :], rsm[:, 1, :]))
            link(nc.vector.tensor_tensor(be(rout[:, 0, :]), be(rout[:, 2, :]), over_e(rsm[:, 2, :]), ALU.mult))
            link(nc.vector.reduce_sum(rsm[:, 3, :], rout[:, 0, :].rearrange("p (b e) -> p e b", e=E), AX_X))
            link(nc.vector.reciprocal(rsm[:, 4, :], rsm[:, 3, :]))
            link(nc.vector.tensor_scalar(rsm[:, 5, :], rsm[:, 4, :], CAPACITY / N, 1.0, ALU.mult, ALU.min))
            link(nc.vector.tensor_tensor(be(rout[:, 3, :]), be(rout[:, 0, :]),
                                         rsm[:, 5, :].unsqueeze(1).broadcast_to([P, B, E]), ALU.mult))
            def largest(i):
                return nc.vector.max(m8[:, i, :], rout[:, 3, i * E:(i + 1) * E])

            def indices(i):
                return nc.vector.max_index(i8[:, i, :], m8[:, i, :], rout[:, 3, i * E:(i + 1) * E])

            largest(0)
            link(largest(1), lambda: (largest(2), largest(3)))
            indices(0)
            indices(1).then_inc(s["top"], 1)
            for i in range(4, B):
                last = largest(i)
            link(last)
            nc.vector.tensor_tensor(rx[:, 0, B * E:], m8[:, :, 1], m8[:, :, 0], ALU.subtract)
            nc.vector.tensor_tensor(be(rx[:, 0, 0:B * E]), be(rout[:, 3, :]),
                                    m8[:, :, 0:1].broadcast_to([P, B, E]), ALU.subtract).then_inc(s["rx2"], 1)
            for i in range(2, B):
                last = indices(i)
            last.then_inc(s["top"], 1)
            dve.wait_ge(s["rexp2"], 1)
            nc.vector.tensor_scalar(rsm[:, 2, :], rx[:, 1, B * E:], 1.0, None, ALU.subtract)
            link(nc.vector.reduce_sum(rsm[:, 0, :], be(rx[:, 1, 0:B * E]), AX_X))
            link(nc.vector.reciprocal(rsm[:, 1, :], rsm[:, 0, :]))
            nc.vector.tensor_tensor(rsm[:, 6, :], rsm[:, 2, :], rsm[:, 1, :], ALU.mult).then_inc(s["rx3"], 1)
            dve.wait_ge(s["half_tanh"], 1)
            nc.vector.tensor_scalar(wk[:, :, 0], rsm[:, 7, :], -0.5, 0.5, ALU.mult, ALU.add)
            nc.vector.tensor_scalar(wk[:, :, 1], rsm[:, 7, :], 0.5, 0.5, ALU.mult, ALU.add).then_inc(s["wkd"], 1)

            def bias2(p):
                dve.wait_ge(s["g2"], 2 * TOP * (p + 1))
                for b in range(2):
                    rows = slice(b * C, (b + 1) * C)
                    last = nc.vector.tensor_tensor(c2[rows, p:p + 1], b2g[rows, p % 2, b, 0:1],
                                                   b2g[rows, p % 2, b, 1:2], ALU.add)
                last.then_inc(s["c2d"], 1)
                dve.wait_ge(s["c2d"], p + 1)

            def evac_z(p):
                dve.wait_ge(s["mm2"], TOP * (p + 1))
                for h in range(2):
                    if h:
                        dve.wait_ge(s["sq3"], 2 * p + 1)
                    cols = slice(h * HALF, (h + 1) * HALF)
                    nc.vector.tensor_scalar(ZS[:, p, cols], y_ps[:, cols], c2[:, p:p + 1], w("gamma"),
                                            ALU.add, ALU.mult).then_inc(s["zs"], 1)

            def rstd3(p):
                dve.wait_ge(s["mom3"], p + 1)
                pm = moments_of(pM)
                nc.vector.tensor_scalar(by_half(v3[:, p, :]), pm[:, 0], RSQRT, RSQRT * EPS_T, ALU.mult,
                                        ALU.add).then_inc(s["red3"], 1)
                dve.wait_ge(s["red3"], p + 1)
                if p == 0:
                    dve.wait_ge(s["pow2"], 2)
                else:
                    dve.wait_ge(s["pow3"], p)
                rsqrt(v3[:, p, :], nwt[:, 0, 0:G2], nwt[:, 1, 0:G2], seed[:, 0:G2], r3[:, p, :], s["pow3"])

            def rows3(p):
                dve.wait_ge(s["rt3"], p + 1)
                if p >= 2:
                    dve.wait_ge(s["rb3"], 2 * (p - 1))
                nc.vector.tensor_copy(RR[:, p % 2, :], ps_rt3[p]).then_inc(s["rr3"], 1)

            def scale_z(p, h):
                dve.wait_ge(s["rb3"], 2 * p + h + 1)
                cols = slice(h * HALF, (h + 1) * HALF)
                nc.vector.tensor_tensor(V[:, p, cols], ZS[:, p, cols], rb3[p][h], ALU.mult).then_inc(s["vv"], 1)

            bias2(0)
            bias2(1)
            for p in range(NP):
                if p < NP - 1:
                    evac_z(p)
                if p >= 1:
                    scale_z(p - 1, 0)
                if 1 <= p < NP - 1:
                    scale_z(p - 1, 1)
                rstd3(p)
                if p == NP - 2:
                    evac_z(NP - 1)
                if p == NP - 1:
                    dve.wait_ge(s["pow3"], NP)
                    dve.wait_ge(s["rt3"], NP - 2)
                    split3(nc.vector, link, p % 2, 1, r3[:, p:p + 1, :], s["s3"])
                rows3(p)
                if p + 2 < NP:
                    bias2(p + 2)
            scale_z(NP - 2, 1)
            scale_z(NP - 1, 0)
            scale_z(NP - 1, 1)
            add_residual(nc.vector, dve, NP - 1, 1)

        @block.tensor
        def _(pe):
            mm = nc.tensor.matmul

            def half(ap, b):
                return ap[b * C:(b + 1) * C]

            def gram(p):
                g, l = p // 2, p % 2
                pe.wait_ge(s["ones"], 1)
                pe.wait_ge(s_ut[p], 1)
                for j in range(CH):
                    last = mm(ps_g[g][:, l * G1:(l + 1) * G1], UT[:, p, j, 1:P + 1], UT[:, p, j, :],
                              start=(j == 0), stop=(j == CH - 1))
                if l:
                    last.then_inc(s["gram"], 1)

            def transpose_u(p):
                pe.wait_ge(s_ut[p], 1)
                if p >= 1:
                    pe.wait_ge(s["u"], p)
                for j in range(CH):
                    last = nc.tensor.transpose(ut[:, j * P:(j + 1) * P], UT[:, p, j, 1:P + 1], cf("ident"))
                last.then_inc(s["tb"], 1)

            def att_p1(g):
                pe.wait_ge(s["gs"], g + 1)
                for l in range(2):
                    for b in range(2):
                        c0 = l * G1 + 1 + b * C
                        mm(half(ps_p1[g][:, l, :], b), half(Gs[:, g, c0:c0 + C], b), half(wTc[:, WK], b),
                           start=True, stop=True)
                        last = mm(half(ps_vb[g][:, l, :], b), half(Gs[:, g, l * G1:l * G1 + 1], b).broadcast_to([C, C]),
                                  half(wTc[:, WK], b), start=True, stop=True)
                last.then_inc(s["p1"], 1)

            def att_s(g):
                pe.wait_ge(s["p1s"], g + 1)
                for l in range(2):
                    for b in range(2):
                        last = mm(half(ps_s[g][:, l, :], b), half(wTc[:, WQ], b), half(p1s[:, g, l, :], b),
                                  start=True, stop=True)
                last.then_inc(s["s_ps"], 1)

            def att_b1(g):
                pe.wait_ge(s["a_sb"], g + 1)
                for l in range(2):
                    for b in range(2):
                        last = mm(half(ps_b1[g][:, l, :], b), half(A[:, g, l, :], b), half(w("woT"), b),
                                  start=True, stop=True)
                last.then_inc(s["b1"], 1)

            def att_mt(g):
                pe.wait_ge(s["b1s"], g + 1)
                for l in range(2):
                    for b in range(2):
                        mm(half(ps_mt[g][:, l, :], b), half(wvc[:, :], b), half(B1s[:, g, l, :], b),
                           start=True, stop=True)
                        last = mm(half(ps_cb[g][:, l:l + 1], b), half(B1s[:, g, l, :], b), half(w("bv"), b),
                                  start=True, stop=True)
                last.then_inc(s["mt"], 1)

            def conv(p):
                pe.wait_ge(s["mts"], p // 2 + 1)
                pe.wait_ge(s["u"], p + 1)
                if p == 0:
                    pe.wait_ge(s["w1l"], 1)
                for h in range(2):
                    if p >= 1:
                        pe.wait_ge(s["t"], 2 * p + h - 1)
                    cols = slice(h * HALF, (h + 1) * HALF)
                    mm(cv[:, cols], MTs[:, p, :], U[:, p, cols], start=True, stop=True).then_inc(s["conv"], 1)

            def moment_rows(bank, k, src):
                for q in range(4):
                    last = mm(bank[32 * q:32 * (q + 1), k * 256:(k + 1) * 256], cf("mean2"),
                              src[:, q * 256:(q + 1) * 256], start=True, stop=True)
                return last

            def moment_columns(bank, n, rw, done):
                for k in range(n):
                    last = nc.tensor.transpose(bank[:, k * P:(k + 1) * P], rw[:, k * P:(k + 1) * P], cf("ident"))
                last.then_inc(done, 1)

            def rows2(p):
                pe.wait_ge(s["t"], 2 * p + 2)
                if p >= 2:
                    pe.wait_ge(s["red2"], p - 1)
                moment_rows(moment_bank[p % 2], 0, T[:, p, :])
                pe.wait_ge(s_sq[p], 1)
                moment_rows(moment_bank[p % 2], 1, SQ[:, p % 2, :]).then_inc(s["row"], 1)

            def columns2(p):
                pe.wait_ge(s["rw"], p + 1)
                moment_columns(moment_bank[p % 2], 4, RW[:, p % 2, :], s["mom"])

            def turn(dst, l):
                return nc.tensor.transpose(dst, R3[:, l, :, :].rearrange("p k g -> p (k g)"), cb("identb"))

            def turn2(g):
                pe.wait_ge(s["r3"], g + 1)
                pe.wait_ge(s["cbs"], 2)
                if g >= 1:
                    pe.wait_ge(s["rr"], g)
                for l in range(2):
                    last = turn(ps_rt2[:, l * P:(l + 1) * P], l)
                last.then_inc(s["rt"], 1)

            def spread(dst, j0, n, p):
                for k in range(n):
                    j = j0 + k
                    last = mm(dst[:, k * P:(k + 1) * P], cb("sel")[0:3 * G2, j * P:(j + 1) * P],
                              RR[:, p % 2, :], start=True, stop=True)
                return last

            def spread2(p):
                pe.wait_ge(s["rr"], p // 2 + 1)
                if p == 0:
                    pe.wait_ge(s["t"], 2 * NP)
                elif p == 1:
                    pe.wait_ge(s["u"], NP)
                else:
                    pe.wait_ge(s["uf"], p - 1)
                spread(rb[p % 2], 0, CH, p).then_inc(s["rb"], 1)

            def spread3(p, h):
                pe.wait_ge(s["rr3"], p + 1)
                if 2 * p + h >= 1 and p < NP - 1:
                    pe.wait_ge(s["vv"], 2 * p + h)
                spread(rb3[p][h], h * CH // 2, CH // 2, p).then_inc(s["rb3"], 1)

            def centre_w2(experts):
                for e in experts:
                    last = mm(ps_w2[:, e * C:(e + 1) * C], w12_sb[C:P, e * F:(e + 1) * F], cf("cend", C, P)[:, 0:C],
                              start=True, stop=True)
                last.then_inc(s["w2p"], 1)

            def warm_up(n):
                for _ in range(n):
                    mm(pM[:, 0:480], cf("ident"), cst[:, 0:480], start=True, stop=True)

            def keep_awake(n, bank=None):
                if bank is None:
                    pe.wait_ge(s["w2v"], 1)
                    bank = ps_w2
                else:
                    pe.wait_ge(s["u"], NP)
                for _ in range(n):
                    mm(bank, cb("identb"), cb("sel")[:, 0:HALF], start=True, stop=True)

            pe.wait_ge(s_cst, 16)
            warm_up(2)
            pe.wait_ge(s_w12, 16)
            for h in range(2):
                last = mm(pC[:, h * HALF:(h + 1) * HALF], cf("cend", 0, C), w12_sb[0:C, h * HALF:(h + 1) * HALF],
                          start=True, stop=True)
            last.then_inc(s["w1p"], 1)
            pe.wait_ge(s_wsm, 16)
            mm(pS[:, 0:3 * C + E], cf("cen2"), w("wT"), start=True, stop=True)
            mm(pS[:, 260:260 + E], cf("cen2"), w("b2T"), start=True, stop=True)
            for b in range(2):
                last = mm(half(pS[:, 300:300 + C], b), half(w("wvT"), b), half(cf("cend"), b)[:, 0:C],
                          start=True, stop=True)
            last.then_inc(s["wcp"], 1)
            warm_up(1)
            pe.wait_ge(s["wcv"], 1)
            pe.wait_ge(s_cstb, 16)
            gram(0)
            gram(1)
            transpose_u(0)
            att_p1(0)
            transpose_u(1)
            att_s(0)
            gram(2)
            att_b1(0)
            transpose_u(2)
            att_mt(0)
            centre_w2(range(0, E // 2))
            conv(0)
            gram(3)
            conv(1)
            att_p1(1)
            transpose_u(3)
            att_s(1)
            rows2(0)
            keep_awake(5, pA[:, 0:HALF])
            att_b1(1)
            rows2(1)
            att_mt(1)
            columns2(0)
            conv(2)
            columns2(1)
            conv(3)
            centre_w2(range(E // 2, E))
            rows2(2)
            rows2(3)
            columns2(2)
            columns2(3)
            turn2(0)
            spread2(0)
            spread2(1)
            keep_awake(5)
            turn2(1)
            spread2(2)
            spread2(3)
            keep_awake(5)
            pe.wait_ge(s["sw"], 1)
            pe.wait_ge(s["onesm"], 1)
            mm(ps_lg, ones_m[:, :], sw[:, :], start=True, stop=True).then_inc(s["lg"], 1)
            keep_awake(18)

            pe.wait_ge(s["w1l"], 1)

            chosen = {}

            def load_experts(step):
                p, k = step // TOP, step % TOP
                if step <= TOP:
                    pe.wait_ge(s["top"], 1 + step // TOP)
                chosen[step] = [nc.tensor.value_load(i8[0:1, 2 * p + b, k:k + 1], min_val=0, max_val=E - 1)
                                for b in range(2)]

            def up(step):
                p, k = step // TOP, step % TOP
                if k == 0:
                    pe.wait_ge(s_st[p], 64)
                experts = chosen.pop(step)
                w1 = w1hl[:, :, :, :].rearrange("p e a f -> p (e a f)")
                for b in range(2):
                    if step >= 1:
                        pe.wait_ge(s["gelu"], 2 * (step - 1) + b + 1)
                    for a in range(2):
                        for h in range(2):
                            cols = slice(h * HALF, (h + 1) * HALF)
                            last = mm(h_ps[b][:, cols], w1[:, bass.ds(experts[b] * 2 * F + a * F, F)],
                                      ST[:, 2 * p + b, cols],
                                      start=(a == 0), stop=(a == 1))
                    last.then_inc(s["mm1"], 1)
                if step + 1 < TOP * NP:
                    load_experts(step + 1)

            def residual3(p):
                if p >= 1:
                    pe.wait_ge(s["zs"], 2 * p)
                    pe.wait_ge(s["sq3"], 2 * p)
                pe.wait_ge(s_st[p], 64)
                for h in range(2):
                    cols = slice(h * HALF, (h + 1) * HALF)
                    for b in range(2):
                        mm(half(y_ps[:, cols], b), cb("cenr"), ST[:, 2 * p + b, cols], start=True, stop=False)

            def down(step, between=None):
                p, k = step // TOP, step % TOP
                if k == 0 and p >= 1:
                    residual3(p)
                pe.wait_ge(s["gelu"], 2 * (step + 1))
                pe.wait_ge(s["g2"], 2 * (step + 1))
                for h in range(2):
                    cols = slice(h * HALF, (h + 1) * HALF)
                    for b in range(2):
                        last = mm(half(y_ps[:, cols], b), w2g[:, p % 2, b, k, :], H[:, step % 2, b, cols],
                                  start=False, stop=(k == TOP - 1))
                    if h == 0 and between:
                        between()
                last.then_inc(s["mm2"], 1)

            def keep_awake_at_end(n):
                for _ in range(n):
                    mm(h_ps[0][:, 0:HALF], cb("identb"), cb("sel")[:, 0:HALF], start=True, stop=True)

            def rows3(p):
                pe.wait_ge(s["sq3"], 2 * p + 2)
                if p >= 1:
                    pe.wait_ge(s["red3"], p)
                moment_rows(pM, 0, SQ[:, p % 2, :]).then_inc(s["row3"], 1)

            def columns3(p):
                pe.wait_ge(s["rw3"], p + 1)
                moment_columns(pM, 2, RW[:, p % 2, :], s["mom3"])

            def turn3(p):
                pe.wait_ge(s["s3"], p + 1)
                if 1 <= p < NP - 1:
                    pe.wait_ge(s["vv"], 2 * p)
                turn(ps_rt3[p], p % 2).then_inc(s["rt3"], 1)

            residual3(0)
            load_experts(0)
            for step in range(TOP * NP + 4):
                q, odd = (step - 5) // TOP, step % TOP
                if step < TOP * NP:
                    up(step)
                if step > TOP * NP and odd and q + 1 < NP:
                    rows3(q + 1)
                if odd and q >= 0:
                    spread3(q, 0)
                if step < TOP * NP and odd and q + 1 >= 0:
                    rows3(q + 1)

                def between():
                    if step > TOP * NP and odd and q + 1 < NP:
                        columns3(q + 1)
                    if odd and q >= 0:
                        spread3(q, 1)
                    if step < TOP * NP and odd and q + 1 >= 0:
                        columns3(q + 1)

                if 1 <= step <= TOP * NP:
                    down(step - 1, between)
                else:
                    between()
                if not odd and 0 <= (step - 4) // TOP < NP:
                    if step >= TOP * NP:
                        keep_awake_at_end(7 if step == TOP * NP else 9)
                    turn3((step - 4) // TOP)


def kernel(x, L0_conv_Wqkv, L0_conv_bqkv, L0_conv_Wout, L0_conv_bout, L0_ffn_Wr, L0_ffn_br, L0_ffn_W1, L0_ffn_b1,
           L0_ffn_W2, L0_ffn_b2, L0_ffn_gamma, L0_ffn_beta):
    import ml_dtypes
    import numpy as np
    import concourse.bacc as bacc
    from concourse.bass_utils import run_bass_kernel_spmd

    def twice(a):
        a = np.asarray(a)
        return np.concatenate([a, a], axis=0)

    def rows(a):
        return np.broadcast_to(np.asarray(a)[None, :], (P, a.shape[0]))

    wqkv, bqkv, wout = np.asarray(L0_conv_Wqkv), np.asarray(L0_conv_bqkv), np.asarray(L0_conv_Wout)
    parts = {
        "wT": twice(np.concatenate([wqkv.T, np.asarray(L0_ffn_Wr)], axis=1)),
        "wvT": twice(wqkv[2 * C:].T), "bk": rows(bqkv[C:2 * C]),
        "woT": twice(wout.T.reshape(D, HEADS, C).transpose(1, 0, 2).reshape(C, C)),
        "b2T": twice(np.asarray(L0_ffn_b2).T), "b1T": np.asarray(L0_ffn_b1).T, "br": rows(L0_ffn_br),
        "bq": twice(bqkv[:C, None]), "bv": twice(bqkv[2 * C:, None]),
        "bout": twice(np.asarray(L0_conv_bout)[:, None]), "gamma": twice(np.asarray(L0_ffn_gamma)[:, None]),
        "beta": twice(np.asarray(L0_ffn_beta)[:, None]),
    }
    small = np.ascontiguousarray(np.concatenate([parts[n] for n, _ in _COLS], axis=1))
    w12 = np.ascontiguousarray(np.concatenate(
        [np.asarray(L0_ffn_W1).transpose(1, 0, 2).reshape(C, E * F),
         np.asarray(L0_ffn_W2).transpose(2, 0, 1).reshape(C, E * F)], axis=0))
    x_tok = np.ascontiguousarray(np.asarray(x).reshape(NP, 2, C, CH, P).transpose(4, 0, 3, 1, 2).reshape(P, NP, N))
    x_cha = np.ascontiguousarray(np.asarray(x).reshape(NP, P, N).transpose(1, 0, 2))

    eye = np.eye(C, dtype=np.float32)
    cen = eye - np.float32(1.0 / C)
    zero = np.zeros((C, C), np.float32)
    head = np.arange(P)[:, None] % C // D
    cons = {
        "ident": np.eye(P, dtype=np.float32), "cen2": np.block([[cen, zero], [zero, cen]]),
        "cend": np.block([[cen, cen], [cen, cen]]),
        "mean2": (np.arange(P)[:, None] // C == np.arange(32)[None, :]).astype(np.float32) / np.float32(C),
        "mask": np.where(head == np.arange(C)[None, :] // D, 0.0, -1e30).astype(np.float32),
    }
    consts = np.ascontiguousarray(np.concatenate([cons[n] for n, _ in _CONS], axis=1))
    sel = np.zeros((P, CH, P), np.float32)
    for k in range(3):
        for j in range(CH):
            for b in range(2):
                sel[k * G2 + 2 * j + b, j, b * C:(b + 1) * C] = 1.0
    conb = {"sel": sel.reshape(P, CH * P), "identb": np.eye(P, dtype=np.float32),
            "cenr": np.concatenate([cen, cen], axis=0) / np.float32(S_U)}
    constb = np.ascontiguousarray(np.concatenate([conb[n] for n, _ in _CONB], axis=1).astype(ml_dtypes.bfloat16))

    nc = bacc.Bacc("TRN2", target_bir_lowering=False, num_devices=1)
    arrays = {"x_tok_dram": x_tok, "x_cha_dram": x_cha, "small_dram": small, "w12_dram": w12,
              "consts_dram": consts, "constb_dram": constb}
    args = [nc.dram_tensor(n, a.shape, mybir.dt.from_np(a.dtype), kind="ExternalInput").ap()
            for n, a in arrays.items()]
    args.append(nc.dram_tensor("out_dram", (P, NP, N), F32, kind="ExternalOutput").ap())
    build_program(nc, *args)
    r = run_bass_kernel_spmd(nc, [arrays], core_ids=[0])
    got = np.asarray(r.results[0]["out_dram"])
    return np.ascontiguousarray(got.transpose(1, 0, 2)).reshape(B, C, 32, 32)
```
